# Optimizing a Trainium2 kernel written in Bass

```python
import numpy as np
import jax
import jax.numpy as jnp

def _softmax(x, axis=-1):
    return jax.nn.softmax(x, axis=axis)

def _gelu(x):
    return jax.nn.gelu(x, approximate=True)

def _silu(x):
    return jax.nn.silu(x)

def _sigmoid(x):
    return jax.nn.sigmoid(x)

def _layernorm(x, axis=-1, eps=1e-05):
    m = jnp.mean(x, axis=axis, keepdims=True)
    v = jnp.var(x, axis=axis, keepdims=True)
    return (x - m) / jnp.sqrt(v + eps)

def _scatter_add(tgt, idx, src, axis=0):
    return tgt.at[idx].add(src)

def _segment_sum(src, seg, n):
    return jax.ops.segment_sum(src, seg, n)
kernel_name = 'mk_recurrent_d1_jaxref_r8_3cf0a1'

def setup_inputs(seed: int=0):
    np.random.seed(seed)
    _w = jnp.asarray

    def _L0_attn_setup():
        import jax, jax.numpy as jnp
        import numpy as np
        D_MODEL = 128
        D_STATE = 64
        D_CONV = 4
        EXPAND = 2
        NGROUPS = 1
        CHUNK = 32
        D_INNER = EXPAND * D_MODEL
        N_HEADS = D_INNER // D_STATE
        HEAD_DIM = D_INNER // N_HEADS
        D_PROJ = 2 * D_INNER + 2 * NGROUPS * D_STATE + N_HEADS
        SSD_SCALE = D_STATE ** (-0.5)

        def _ssd_chunked(xh, A, Bm, Cm, dt):
            Bsz, T, H, P = xh.shape
            G, N = (Bm.shape[-2], Bm.shape[-1])
            L = min(CHUNK, T)
            nC = T // L
            rep = H // G
            x_ = xh.reshape(Bsz, nC, L, H, P)
            B_ = Bm.reshape(Bsz, nC, L, G, N)
            C_ = Cm.reshape(Bsz, nC, L, G, N)
            dt_ = dt.reshape(Bsz, nC, L, H)
            log_dA = A * dt_
            cum = jnp.cumsum(log_dA, axis=2)
            causal = jnp.tril(jnp.ones((L, L), bool))[None, None, :, :, None]
            ldm = cum[:, :, :, None, :] - cum[:, :, None, :, :]
            decay = jnp.exp(jnp.where(causal, ldm, -jnp.inf))
            scores = jnp.einsum('bcign,bcjgn->bcijg', C_, B_) * SSD_SCALE
            scores = jnp.repeat(scores, rep, axis=-1) * decay
            x_dt = x_ * dt_[..., None]
            y_intra = jnp.einsum('bcijh,bcjhp->bcihp', scores, x_dt)
            chunk_decay = jnp.exp(cum[:, :, -1, :])
            decay_to_end = jnp.exp(cum[:, :, -1:, :] - cum)
            B_exp = jnp.repeat(B_, rep, axis=-2)
            delta_h = jnp.einsum('bclh,bclhp,bclhn->bchpn', decay_to_end, x_dt, B_exp)

            def step(states, inp):
                cd, dh = inp
                return (cd[:, :, None, None] * states + dh, states)
            init = jnp.zeros((Bsz, H, P, N), jnp.float32)
            _, all_states = jax.lax.scan(step, init, (jnp.moveaxis(chunk_decay, 1, 0), jnp.moveaxis(delta_h, 1, 0)))
            all_states = jnp.moveaxis(all_states, 0, 1)
            C_exp = jnp.repeat(C_, rep, axis=-2)
            decay_from_start = jnp.exp(cum)
            y_inter = jnp.einsum('bcihn,bchpn->bcihp', C_exp, all_states)
            y_inter = y_inter * (decay_from_start[..., None] * SSD_SCALE)
            return (y_intra + y_inter).reshape(Bsz, T, H, P)
        key = jax.random.key(seed)
        ks = jax.random.split(key, 6)
        Bsz, T = (2, 256)
        x = jax.random.normal(ks[0], (Bsz, T, D_MODEL), jnp.float32)
        W_in = jax.random.normal(ks[1], (D_PROJ, D_MODEL), jnp.float32) * D_MODEL ** (-0.5)
        conv_w = jax.random.normal(ks[2], (D_INNER, 1, D_CONV), jnp.float32) * D_CONV ** (-0.5)
        A_log = jax.random.normal(ks[3], (N_HEADS,), jnp.float32) * 0.1
        dt_bias = jax.random.normal(ks[4], (N_HEADS,), jnp.float32) * 0.1
        W_out = jax.random.normal(ks[5], (D_MODEL, D_INNER), jnp.float32) * D_INNER ** (-0.5)
        return {'x': x, 'W_in': W_in, 'conv_w': conv_w, 'A_log': A_log, 'dt_bias': dt_bias, 'W_out': W_out}
    _L0_attn_in = _L0_attn_setup()

    def _L0_ffn_setup():
        import jax, jax.numpy as jnp
        import numpy as np
        TOP_K = 8
        key = jax.random.key(seed)
        ks = jax.random.split(key, 6)
        B, S, D, F, E = (2, 128, 128, 64, 64)
        x = jax.random.normal(ks[0], (B, S, D), dtype=jnp.float32)
        centroids = jax.random.normal(ks[1], (E, D), dtype=jnp.float32) * 0.05
        expert_biases = jnp.zeros((E,), dtype=jnp.float32)
        Ws_up = jax.random.normal(ks[2], (D, F), dtype=jnp.float32) / np.sqrt(D)
        Ws_down = jax.random.normal(ks[3], (F, D), dtype=jnp.float32) / np.sqrt(F)
        W_up = jax.random.normal(ks[4], (E, D, F), dtype=jnp.float32) / np.sqrt(D)
        W_down = jax.random.normal(ks[5], (E, F, D), dtype=jnp.float32) / np.sqrt(F)
        return {'x': x, 'centroids': centroids, 'expert_biases': expert_biases, 'Ws_up': Ws_up, 'Ws_down': Ws_down, 'W_up': W_up, 'W_down': W_down}
    _L0_ffn_in = _L0_ffn_setup()
    _d = {'L0_attn_x': _L0_attn_in['x'], 'L0_attn_W_in': _L0_attn_in['W_in'], 'L0_attn_conv_w': _L0_attn_in['conv_w'], 'L0_attn_A_log': _L0_attn_in['A_log'], 'L0_attn_dt_bias': _L0_attn_in['dt_bias'], 'L0_attn_W_out': _L0_attn_in['W_out'], 'L0_ffn_centroids': _L0_ffn_in['centroids'], 'L0_ffn_expert_biases': _L0_ffn_in['expert_biases'], 'L0_ffn_Ws_up': _L0_ffn_in['Ws_up'], 'L0_ffn_Ws_down': _L0_ffn_in['Ws_down'], 'L0_ffn_W_up': _L0_ffn_in['W_up'], 'L0_ffn_W_down': _L0_ffn_in['W_down']}
    _x0 = _d['L0_attn_x']
    _d['L0_attn_x'] = jax.random.normal(jax.random.fold_in(jax.random.key(seed), 1), (8, 512, 128), dtype=_x0.dtype)
    del _x0
    return _d

def reference(L0_attn_x, L0_attn_W_in, L0_attn_conv_w, L0_attn_A_log, L0_attn_dt_bias, L0_attn_W_out, L0_ffn_centroids, L0_ffn_expert_biases, L0_ffn_Ws_up, L0_ffn_Ws_down, L0_ffn_W_up, L0_ffn_W_down):

    def _L0_attn_ref(x, W_in, conv_w, A_log, dt_bias, W_out):
        import jax, jax.numpy as jnp
        import numpy as np
        D_MODEL = 128
        D_STATE = 64
        D_CONV = 4
        EXPAND = 2
        NGROUPS = 1
        CHUNK = 32
        D_INNER = EXPAND * D_MODEL
        N_HEADS = D_INNER // D_STATE
        HEAD_DIM = D_INNER // N_HEADS
        D_PROJ = 2 * D_INNER + 2 * NGROUPS * D_STATE + N_HEADS
        SSD_SCALE = D_STATE ** (-0.5)

        def _ssd_chunked(xh, A, Bm, Cm, dt):
            Bsz, T, H, P = xh.shape
            G, N = (Bm.shape[-2], Bm.shape[-1])
            L = min(CHUNK, T)
            nC = T // L
            rep = H // G
            x_ = xh.reshape(Bsz, nC, L, H, P)
            B_ = Bm.reshape(Bsz, nC, L, G, N)
            C_ = Cm.reshape(Bsz, nC, L, G, N)
            dt_ = dt.reshape(Bsz, nC, L, H)
            log_dA = A * dt_
            cum = jnp.cumsum(log_dA, axis=2)
            causal = jnp.tril(jnp.ones((L, L), bool))[None, None, :, :, None]
            ldm = cum[:, :, :, None, :] - cum[:, :, None, :, :]
            decay = jnp.exp(jnp.where(causal, ldm, -jnp.inf))
            scores = jnp.einsum('bcign,bcjgn->bcijg', C_, B_) * SSD_SCALE
            scores = jnp.repeat(scores, rep, axis=-1) * decay
            x_dt = x_ * dt_[..., None]
            y_intra = jnp.einsum('bcijh,bcjhp->bcihp', scores, x_dt)
            chunk_decay = jnp.exp(cum[:, :, -1, :])
            decay_to_end = jnp.exp(cum[:, :, -1:, :] - cum)
            B_exp = jnp.repeat(B_, rep, axis=-2)
            delta_h = jnp.einsum('bclh,bclhp,bclhn->bchpn', decay_to_end, x_dt, B_exp)

            def step(states, inp):
                cd, dh = inp
                return (cd[:, :, None, None] * states + dh, states)
            init = jnp.zeros((Bsz, H, P, N), jnp.float32)
            _, all_states = jax.lax.scan(step, init, (jnp.moveaxis(chunk_decay, 1, 0), jnp.moveaxis(delta_h, 1, 0)))
            all_states = jnp.moveaxis(all_states, 0, 1)
            C_exp = jnp.repeat(C_, rep, axis=-2)
            decay_from_start = jnp.exp(cum)
            y_inter = jnp.einsum('bcihn,bchpn->bcihp', C_exp, all_states)
            y_inter = y_inter * (decay_from_start[..., None] * SSD_SCALE)
            return (y_intra + y_inter).reshape(Bsz, T, H, P)
        Bsz, T, _ = x.shape
        proj = jnp.einsum('btd,pd->btp', x, W_in)
        z = proj[..., :D_INNER]
        x_conv = proj[..., D_INNER:2 * D_INNER]
        o = 2 * D_INNER
        Bm = proj[..., o:o + NGROUPS * D_STATE].reshape(Bsz, T, NGROUPS, D_STATE)
        Cm = proj[..., o + NGROUPS * D_STATE:o + 2 * NGROUPS * D_STATE].reshape(Bsz, T, NGROUPS, D_STATE)
        dt_raw = proj[..., o + 2 * NGROUPS * D_STATE:]
        xc = jax.lax.conv_general_dilated(jnp.transpose(x_conv, (0, 2, 1)), conv_w, window_strides=(1,), padding=[(D_CONV - 1, 0)], dimension_numbers=('NCH', 'OIH', 'NCH'), feature_group_count=D_INNER)
        xc = jax.nn.silu(jnp.transpose(xc, (0, 2, 1)))
        A = -jnp.exp(A_log)
        dt = jnp.clip(jax.nn.softplus(dt_raw + dt_bias), 0.0001, 0.5)
        xh = xc.reshape(Bsz, T, N_HEADS, HEAD_DIM)
        y = _ssd_chunked(xh, A, Bm, Cm, dt).reshape(Bsz, T, D_INNER)
        eps = jnp.finfo(jnp.float32).eps
        y = y * jax.lax.rsqrt(jnp.mean(y * y, axis=-1, keepdims=True) + eps)
        y = y * jax.nn.silu(z)
        return jnp.einsum('bti,di->btd', y, W_out)

    def _L0_ffn_ref(x, centroids, expert_biases, Ws_up, Ws_down, W_up, W_down):
        import jax, jax.numpy as jnp
        import numpy as np
        TOP_K = 8
        B, S, D = x.shape
        E = centroids.shape[0]
        T = B * S
        xf = x.reshape(T, D)
        shared = jax.nn.silu(xf @ Ws_up) @ Ws_down
        aff = xf @ centroids.T
        biased = aff + expert_biases
        _, idx = jax.lax.top_k(biased, TOP_K)
        sel = jnp.take_along_axis(aff, idx, axis=1)
        w = jax.nn.sigmoid(sel)
        w = w / (jnp.sum(w, axis=-1, keepdims=True) + 1e-08)
        cw = jnp.zeros((T, E), dtype=x.dtype).at[jnp.arange(T)[:, None], idx].add(w)
        h = jax.nn.silu(jnp.einsum('td,edf->etf', xf, W_up))
        y = jnp.einsum('etf,efd->etd', h, W_down)
        routed = jnp.einsum('etd,te->td', y, cw)
        return (shared + routed).reshape(B, S, D)
    x = L0_attn_x
    xn = _layernorm(x, axis=-1)
    s = _L0_attn_ref(xn, L0_attn_W_in, L0_attn_conv_w, L0_attn_A_log, L0_attn_dt_bias, L0_attn_W_out)
    g = _silu(_L0_ffn_ref(xn, L0_ffn_centroids, L0_ffn_expert_biases, L0_ffn_Ws_up, L0_ffn_Ws_down, L0_ffn_W_up, L0_ffn_W_down))
    x = x + s * g
    return x

_drawn_inputs = setup_inputs


def setup_inputs(seed=0):
    import zlib

    import numpy as np

    out = dict(_drawn_inputs(seed))
    spreads = {'L0_ffn_expert_biases': (0.0, 0.1)}
    factors = {'L0_attn_A_log': 2.809, 'L0_attn_dt_bias': 8.0}
    for name, (base, spread) in spreads.items():
        noise = np.random.default_rng([zlib.crc32(name.encode()), seed]).standard_normal(out[name].shape)
        drawn = base * np.exp(spread * noise) if base else spread * noise
        out[name] = jnp.asarray(drawn.astype(out[name].dtype))
    for name, factor in factors.items():
        out[name] = (out[name] * factor).astype(out[name].dtype)
    return out
```

```python
from contextlib import ExitStack

import concourse.bass as bass
from concourse import mybir

F32 = mybir.dt.float32
F32R = mybir.dt.float32r
ALU = mybir.AluOpType
ACT = mybir.ActivationFunctionType
AX_X = mybir.AxisListType.X

P = 128
LOWEST = -3.4028234e38
LN_EPS = 1e-5
RMS_EPS = 1.1920929e-07
DT_CAP = 20.0
DT_MIN, DT_MAX = 1e-4, 0.5
RING = 3


class Signal:

    def __init__(self, sem, per):
        self.sem, self.per = sem, per

    def start(self, eng):
        eng.sem_inc(self.sem, self.per)

    def wait(self, eng, b, k=None):
        k = self.per - 1 if k is None else k
        eng.wait_ge(self.sem, b * self.per + (self.per + k + 1))

    def wait_previous(self, eng, b, k=None):
        k = self.per - 1 if k is None else k
        eng.wait_ge(self.sem, b * self.per + (k + 1))


def build(nc, x, w_proj, w_out_t, conv_w, rows, w_up, w_down, ws_up, ws_down, out):
    NB, T, D = x.shape
    J = T // P
    E = rows.shape[1] - 8
    H = 4
    DI = 2 * D
    HP = DI // H
    N = (w_proj.shape[1] - 2 * DI - H - E) // 3
    F = ws_up.shape[1]
    NP = E // 2
    G = DI // P
    K = 4
    C_SCALE = float(N) ** -0.5
    TOK = DI + N + H + E
    BTD = N + H + E
    assert D == P and HP * H == DI and 2 * F == P and N == 64

    ctx = ExitStack()
    with ctx:
        def sb(name, shape, dt=F32):
            return ctx.enter_context(nc.sbuf_tensor(name, shape, dt))

        def sem(name):
            return ctx.enter_context(nc.semaphore(name))

        def signal(name, per):
            return Signal(sem(name), per)

        up_hi, up_lo = sb("up_hi", [P, NP + 1, P], F32R), sb("up_lo", [P, NP + 1, P], F32R)
        dn_hi, dn_lo = sb("dn_hi", [P, NP + 1, D], F32R), sb("dn_lo", [P, NP + 1, D], F32R)
        wp_hi, wp_lo = sb("wp_hi", [P, w_proj.shape[1]], F32R), sb("wp_lo", [P, w_proj.shape[1]], F32R)
        w_out_sb = sb("w_out_sb", [P, G, D])
        conv_sb = sb("conv_sb", [P, G, K])
        rows_sb = sb("rows_sb", [P, E + 8])
        neg_a = sb("neg_a", [P, H])
        ident = sb("ident", [P, P])
        upper = sb("upper", [P, P])
        upper_r = sb("upper_r", [P, P], F32R)
        stair = sb("stair", [P, E, F], F32R)
        minus_half = sb("minus_half", [P, J])
        XH, XL = sb("XH", [P, 2, T], F32R), sb("XL", [P, 2, T], F32R)
        CW = sb("CW", [P, 2, T], F32R)
        S = sb("S", [P, 2, J * D])
        x_tok = sb("x_tok", [P, J, D])
        stats = sb("stats", [P, J, 6])
        mv = sb("mv", [P, J, 2])
        var_e = sb("var_e", [P, J])
        rstd = sb("rstd", [P, J])
        xh, xl = sb("xh", [P, T], F32R), sb("xl", [P, T], F32R)
        sz = sb("sz", [P, J, DI])
        btd = sb("btd", [P, J, BTD])
        xraw = sb("xraw", [P, G, T + K - 1])
        xconv = sb("xconv", [P, 2, T])
        xc = sb("xc", [P, G, T])
        bt, ct = sb("bt", [N, T]), sb("ct", [N, T])
        dtv = sb("dtv", [P, J, H])
        dtu, dtl, dtw = sb("dtu", [P, J, H]), sb("dtl", [P, J, H]), sb("dtw", [P, J, H])
        dtr, dt_ = sb("dtr", [P, J, H]), sb("dt_", [P, J, H])
        da = sb("da", [P, J, H])
        da_hi, da_lo = sb("da_hi", [P, J, H], F32R), sb("da_lo", [P, J, H], F32R)
        ncum, ecum = sb("ncum", [P, J, H]), sb("ecum", [P, J, H])
        cend, cdec = sb("cend", [P, J, H]), sb("cdec", [P, J, H])
        decay = sb("decay", [P, J, H, P])
        biased, top8, replaced = sb("biased", [P, J, E]), sb("top8", [P, J, 8]), sb("replaced", [P, J, E])
        sig = sb("sig", [P, J, E])
        wsum, wrec = sb("wsum", [P, J]), sb("wrec", [P, J])
        cw_cat = sb("cw_cat", [P, J, 2, E])
        smask = sb("smask", [P, 2, P])
        mix = sb("mix", [P, 2, H, P])
        xdt, xw = sb("xdt", [P, 2, DI]), sb("xw", [P, 2, DI])
        yint, y = sb("yint", [P, 2, DI]), sb("y", [P, 2, DI])
        ysq, ss, rs = sb("ysq", [P, DI]), sb("ss", [P, J]), sb("rs", [P, J])
        sse = sb("sse", [P, J])
        yg = sb("yg", [P, 2, DI])
        ygt = sb("ygt", [P, 2, DI])
        state, state_d = sb("state", [N, J - 1, DI]), sb("state_d", [N, J - 2, DI])
        hid = sb("hid", [P, 2, T])
        prod = sb("prod", [P, 2, T])
        ph, pl = sb("ph", [P, 2, T], F32R), sb("pl", [P, 2, T], F32R)
        gate_t = sb("gate_t", [P, T])
        x_res = sb("x_res", [P, J, D])
        fin = sb("fin", [P, J, D])

        stage_a = decay[:, :, :, :].rearrange("p j h t -> p (j h t)")

        bank = [ctx.enter_context(nc.psum_tensor(f"bank{i}", [P, 512], F32)) for i in range(8)]
        U_BANK, C_BANK, Y_BANK = (3, 4), (5, 6), 7

        FILLS = [("xnt", 0)] + [("tok", j) for j in range(J)] + [("conv", g) for g in range(G)]
        FILLS += [("bc", 0), ("cum", 0)] + [("cumb", j) for j in range(J)] + [("cwt", 0)]
        FILLS += [("xct", 0), ("score", 0), ("xct", 1), ("score", 1)]
        for j in range(J):
            FILLS += [("y", j)]
            if j + 1 < J:
                FILLS += [("delta", j)]
            if j:
                FILLS += [("ygt", j - 1), ("outp", j - 1)]
            if j + 2 < J:
                FILLS += [("xct", j + 2), ("score", j + 2)]
        FILLS += [("ygt", J - 1), ("outp", J - 1)]
        place = {f: n for n, f in enumerate(FILLS)}
        uses = [len(FILLS[r::RING]) for r in range(RING)]
        per = {}
        for name, _ in FILLS:
            per[name] = per.get(name, 0) + 1
        filled = {name: signal(f"{name}_in_psum", n) for name, n in per.items()}
        bank_free = [signal(f"bank{r}_free", uses[r]) for r in range(RING)]

        def bank_of(name, k=0):
            return bank[place[name, k] % RING]

        def free_of(name, k=0):
            return bank_free[place[name, k] % RING].sem

        def wait_bank(pe, b, name, k=0):
            n = place[name, k]
            r, m = n % RING, n // RING
            if m:
                bank_free[r].wait(pe, b, m - 1)
            else:
                bank_free[r].wait_previous(pe, b)

        s_weights = [sem(f"weights_{i}_landed") for i in range(10)]
        s_const = sem("constants_made")
        s_split_hi, s_split_lo = sem("weight_high_parts_made"), sem("weight_low_parts_made")
        s_setup = sem("setup_made")
        s_passed = sem("lone_waits_passed")
        x_landed = sem("x_landed")
        stats_ready = signal("stats_ready", 2 * J)
        var_ready, rstd_ready = signal("var_ready", 1), signal("rstd_ready", 1)
        xn_ready = signal("xn_ready", J)
        xh_ready, xl_ready = signal("xh_ready", 1), signal("xl_ready", 1)
        kept_x = signal("xh_xl_kept", 2)
        sz_ready, btd_ready = signal("silu_z_ready", J), signal("btd_ready", J)
        xraw_ready = signal("xraw_ready", G)
        bt_ready, ct_ready = signal("bt_ready", 1), signal("ct_ready", 1)
        tap_done = signal("conv_tap_done", G * K)
        xc_ready = signal("xc_ready", G)
        dt_step, dt_exp, dt_ln = signal("dt_step_done", 9), signal("dt_exp_ready", 1), signal("dt_ln_ready", 1)
        ncum_ready, ecum_ready = signal("ncum_ready", 1), signal("ecum_ready", 1)
        arg_ready = signal("decay_argument_ready", J)
        cdec_ready, decay_ready = signal("chunk_decay_ready", 1), signal("decay_ready", J)
        da_step, arg_part, cw_part = signal("da_step_done", 3), signal("decay_argument_part_done", (H + 1) * J), signal("cw_part_done", 2)
        biased_ready, top8_ready, replaced_ready = signal("biased_ready", 1), signal("top8_ready", J), signal("replaced_ready", J)
        affexp_ready, route_step = signal("affinity_exp_ready", 1), signal("route_step_done", 9)
        cw_kept = signal("cw_kept", 1)
        smask_ready, mix_ready = signal("masked_scores_ready", J), signal("mix_ready", J)
        xdt_ready, xw_ready = signal("xdt_ready", J), signal("xw_ready", J)
        yint_ready, y_ready = signal("y_inter_ready", J), signal("y_ready", J)
        ss_ready, rs_ready = signal("y_square_sum_ready", J), signal("y_rstd_ready", 2 * J)
        yg_ready, ygt_ready = signal("gated_y_ready", J), signal("gated_y_t_ready", J)
        stated_ready, state_ready = signal("state_decayed", J), signal("state_ready", J)
        s_kept = signal("s_kept", J)
        NQ = NP + 1
        u_filled, u_read = signal("up_in_psum", NQ), signal("hidden_ready", NQ)
        c_filled = signal("weights_in_psum", NP)
        prod_ready = signal("weighted_hidden_ready", NQ)
        ph_ready, pl_ready = signal("high_part_ready", NQ), signal("low_part_ready", NQ)
        down_done = signal("down_product_done", NQ)
        gate_ready = signal("gate_t_ready", 1)
        g_filled = signal("gate_in_psum", 1)
        fin_step, fin_read = signal("result_step_done", 2), signal("result_stored", 1)
        xres_landed = sem("x_residual_landed")
        stored = sem("result_landed_in_dram")

        Y_SLOT = [23, 25, 28, 31]

        block = ctx.enter_context(nc.Block())

        def at(tile, b):
            return tile[:, bass.ds(b % 2, 1), :].rearrange("p a t -> p (a t)")

        def apart(eng):
            eng.sem_inc(s_passed, 1)

        def advance(mixer, p):
            while mixer.slot <= p:
                mixer.slot = next(mixer.steps, 10 ** 6)

        class Mixer:
            def __init__(self, steps):
                self.steps, self.slot = steps, next(steps)

        def run(eng, front, experts):
            advance(Mixer(front(0)), 10 ** 5)
            with eng.Fori(1, NB) as b:
                mixer = Mixer(front(b))
                experts(b - 1, mixer)
                advance(mixer, 10 ** 5)
            experts(NB - 1, None)

        def first(b):
            return isinstance(b, int) and b == 0

        def step(mixer, p):
            if mixer:
                advance(mixer, p)

        x_view = x.rearrange("b (j p) d -> b p j d", p=P)
        out_view = out.rearrange("b (j p) d -> b p j d", p=P)

        def dram_at(view, b):
            return view[bass.ds(b, 1), :, :, :].rearrange("a p j d -> (a p) j d")

        C_CONV, C_BC = TOK, TOK + DI
        WP = w_proj.shape[1]
        QUARTER = NP // 4

        def pieces():
            for q in range(4):
                sl = slice(q * QUARTER * P, (q + 1) * QUARTER * P)
                yield w_up[:, sl], up_hi[:, q * QUARTER:(q + 1) * QUARTER, :], up_lo[:, q * QUARTER:(q + 1) * QUARTER, :]
            for q in range(4):
                sl = slice(q * QUARTER * D, (q + 1) * QUARTER * D)
                yield w_down[:, sl], dn_hi[:, q * QUARTER:(q + 1) * QUARTER, :], dn_lo[:, q * QUARTER:(q + 1) * QUARTER, :]

        W4 = QUARTER * P
        land = [decay[:, :, :, :].rearrange("p j h t -> p (j h t)")[:, 0:W4], decay[:, :, :, :].rearrange("p j h t -> p (j h t)")[:, W4:2 * W4]]
        SPLITS = list(pieces())
        small = prod[:, :, :].rearrange("p a t -> p (a t)")

        @block.sync
        def _(sp):
            def load(b):
                filled["xnt"].wait_previous(sp, b)
                sp.dma_start(x_tok[:, :, :], dram_at(x_view, b)).then_inc(x_landed, 16)

            def finish(b):
                fin_step.wait_previous(sp, b)
                sp.dma_start(x_res[:, :, :], dram_at(x_view, b)).then_inc(xres_landed, 16)
                fin_step.wait(sp, b)
                sp.dma_start(dram_at(out_view, b), fin[:, :, :]).then_inc(stored, 16)
                sp.wait_ge(stored, b * 16 + 16)
                sp.sem_inc(fin_read.sem, 1)

            sp.dma_start(small[:, 0:WP], w_proj).then_inc(s_weights[8], 16)
            load(0)
            load(1)
            with sp.Fori(1, NB - 1) as b:
                load(b + 1)
                finish(b - 1)
            finish(NB - 2)
            finish(NB - 1)

        @block.gpsimd
        def _(pool):
            for s in (var_ready, rstd_ready, kept_x, xw_ready, mix_ready, yg_ready, rs_ready, stated_ready):
                s.start(pool)
            pool.memset(ident[:, :], 0.0).then_inc(s_const, 1)
            pool.memset(upper[:, :], 1.0).then_inc(s_const, 1)
            pool.memset(stair[:, :, :].rearrange("p e f -> p (e f)").bitcast(F32), 0.0).then_inc(s_const, 1)
            pool.memset(minus_half[:, :], -0.5).then_inc(s_const, 1)
            pool.memset(xraw[:, :, 0:K - 1], 0.0).then_inc(s_const, 1)
            pool.wait_ge(s_const, 5)
            pool.affine_select(out=ident[:, :], in_=ident[:, :], compare_op=ALU.not_equal, fill=1.0, base=0,
                               pattern=[[-1, P]], channel_multiplier=1).then_inc(s_const, 1)
            pool.affine_select(out=upper[:, :], in_=upper[:, :], compare_op=ALU.is_ge, fill=0.0, base=0,
                               pattern=[[1, P]], channel_multiplier=-1).then_inc(s_const, 1)
            pool.affine_select(out=stair[:, :, :], in_=stair[:, :, :].bitcast(F32), compare_op=ALU.not_equal, fill=1.0, base=0,
                               pattern=[[-1, E], [0, F]], channel_multiplier=1).then_inc(s_const, 1)
            pool.wait_ge(s_const, 8)
            pool.affine_select(out=stair[:, :, :], in_=stair[:, :, :].bitcast(F32), compare_op=ALU.not_equal, fill=1.0, base=-E,
                               pattern=[[-1, E], [0, F]], channel_multiplier=1).then_inc(s_const, 1)
            def front(b):
                stats_ready.wait(pool, b)
                apart(pool)
                pool.tensor_scalar(var_e[:, :], mv[:, :, 1], LN_EPS, None, ALU.add).then_inc(var_ready.sem, 1)
                var_ready.wait(pool, b)
                pool.tensor_tensor(rstd[:, :], var_e[:, :], minus_half[:, :], ALU.pow).then_inc(rstd_ready.sem, 1)
                if not first(b):
                    gate_ready.wait_previous(pool, b - 1)
                xh_ready.wait(pool, b)
                pool.tensor_copy(at(XH, b), xh[:, :]).then_inc(kept_x.sem, 1)
                xl_ready.wait(pool, b)
                pool.tensor_copy(at(XL, b), xl[:, :]).then_inc(kept_x.sem, 1)
                for j in range(J):
                    q = j % 2
                    decay_ready.wait(pool, b, j)
                    xdt_ready.wait(pool, b, j)
                    pool.tensor_tensor(xw[:, q, :].rearrange("p (h n) -> p h n", h=H),
                                       xdt[:, q, :].rearrange("p (h n) -> p h n", h=H),
                                       decay[:, j, :, P - 1:P].to_broadcast([P, H, HP]), ALU.mult).then_inc(xw_ready.sem, 1)
                    smask_ready.wait(pool, b, j)
                    pool.tensor_tensor(mix[:, q, :, :], decay[:, j, :, :],
                                       smask[:, q, :].unsqueeze(1).to_broadcast([P, H, P]), ALU.mult).then_inc(mix_ready.sem, 1)
                    if 0 < j < J - 1:
                        cdec_ready.wait(pool, b)
                        state_ready.wait(pool, b, j - 1)
                        pool.tensor_tensor(state_d[:, j - 1, :].rearrange("p (h n) -> p h n", h=H),
                                           state[:, j - 1, :].rearrange("p (h n) -> p h n", h=H),
                                           cdec[0:N, j, :].unsqueeze(2).to_broadcast([N, H, HP]), ALU.mult)\
                            .then_inc(stated_ready.sem, 1)
                    y_ready.wait(pool, b, j)
                    sz_ready.wait(pool, b, j)
                    pool.tensor_tensor(yg[:, q, :], y[:, q, :], sz[:, j, :], ALU.mult).then_inc(yg_ready.sem, 1)
                    ss_ready.wait(pool, b, j)
                    apart(pool)
                    pool.tensor_scalar(sse[:, j:j + 1], ss[:, j:j + 1], 1.0 / DI, RMS_EPS, ALU.mult, ALU.add)\
                        .then_inc(rs_ready.sem, 1)
                    rs_ready.wait(pool, b, 2 * j)
                    pool.tensor_tensor(rs[:, j:j + 1], sse[:, j:j + 1], minus_half[:, 0:1], ALU.pow).then_inc(rs_ready.sem, 1)
                pool.sem_inc(stated_ready.sem, 2)

            front(0)
            with pool.Fori(1, NB) as b:
                front(b)

        @block.scalar
        def _(act):
            for s in (xh_ready, sz_ready, btd_ready, xraw_ready, bt_ready, ct_ready, xc_ready, dt_exp, dt_ln,
                      ecum_ready, cdec_ready, decay_ready, affexp_ready, cw_kept, ss_ready, ygt_ready,
                      u_read, ph_ready, gate_ready):
                s.start(act)
            act.dma_start(rows_sb[:, :], rows).then_inc(s_weights[0], 16)
            act.dma_start(conv_sb[:, :, :], conv_w).then_inc(s_weights[1], 16)
            act.dma_start(w_out_sb[:, :, :], w_out_t).then_inc(s_weights[2], 16)
            act.dma_start(hid[:, 0, 0:F], ws_up).then_inc(s_weights[3], 16)
            act.dma_start(hid[0:F, 1, 0:D], ws_down).then_inc(s_weights[4], 16)
            for n, (src, hi, lo) in enumerate(SPLITS):
                if n >= 2:
                    act.wait_ge(s_split_lo, n - 1)
                act.dma_start(land[n % 2], src).then_inc(s_weights[5 + n % 2], 16)
                if n:
                    act.wait_ge(s_weights[5 + (n - 1) % 2], 16 * ((n - 1) // 2 + 1))
                    act.activation(SPLITS[n - 1][1].rearrange("p a t -> p (a t)"), land[(n - 1) % 2], ACT.Copy)\
                        .then_inc(s_split_hi, 1)
            n = len(SPLITS)
            act.wait_ge(s_weights[5 + (n - 1) % 2], 16 * ((n - 1) // 2 + 1))
            act.activation(SPLITS[n - 1][1].rearrange("p a t -> p (a t)"), land[(n - 1) % 2], ACT.Copy).then_inc(s_split_hi, 1)
            act.wait_ge(s_weights[8], 16)
            act.activation(wp_hi[:, :], small[:, 0:WP], ACT.Copy).then_inc(s_split_hi, 1)
            act.wait_ge(s_weights[3], 16)
            act.activation(up_hi[:, NP, 0:F], hid[:, 0, 0:F], ACT.Copy).then_inc(s_split_hi, 1)
            act.wait_ge(s_weights[4], 16)
            act.activation(dn_hi[0:F, NP, :], hid[0:F, 1, 0:D], ACT.Copy).then_inc(s_split_hi, 1)
            act.wait_ge(s_const, 9)
            act.activation(upper_r[:, :], upper[:, :], ACT.Copy).then_inc(s_setup, 1)
            act.sem_inc(s_setup, 1)
            act.wait_ge(s_weights[0], 16)
            act.activation(neg_a[:, :], rows_sb[:, E + 4:E + 8], ACT.Exp).then_inc(s_setup, 1)

            def front(b):
                yield 3
                filled["xnt"].wait(act, b)
                filled["bc"].wait_previous(act, b)
                if not first(b):
                    kept_x.wait_previous(act, b)
                act.activation(xh[:, :], bank_of("xnt")[:, :], ACT.Copy).then_inc(xh_ready.sem, 1)
                for j in range(J):
                    yield 6 + j
                    filled["tok"].wait(act, b, j)
                    ps = bank_of("tok", j)
                    yg_ready.wait_previous(act, b, j)
                    act.activation(sz[:, j, :], ps[:, 0:DI], ACT.Silu).then_inc(sz_ready.sem, 1)
                    route_step.wait_previous(act, b)
                    act.activation(btd[:, j, :], ps[:, DI:TOK], ACT.Copy).then_inc(btd_ready.sem, 1)
                    sz_ready.wait(act, b, j)
                    btd_ready.wait(act, b, j)
                    act.sem_inc(free_of("tok", j), 1)
                for g in range(G):
                    yield 10 + g
                    filled["conv"].wait(act, b, g)
                    tap_done.wait_previous(act, b)
                    act.activation(xraw[:, g, K - 1:], bank_of("conv", g)[:, :], ACT.Copy).then_inc(xraw_ready.sem, 1)
                    xraw_ready.wait(act, b, g)
                    act.sem_inc(free_of("conv", g), 1)
                yield 12
                filled["bc"].wait(act, b)
                filled["score"].wait_previous(act, b)
                filled["y"].wait_previous(act, b)
                act.activation(bt[:, :], bank_of("bc")[0:N, :], ACT.Copy).then_inc(bt_ready.sem, 1)
                act.activation(ct[:, :], bank_of("bc")[N:2 * N, :], ACT.Copy, scale=C_SCALE).then_inc(ct_ready.sem, 1)
                bt_ready.wait(act, b)
                ct_ready.wait(act, b)
                act.sem_inc(free_of("bc"), 1)
                for g in range(G):
                    yield 14 + 2 * g
                    tap_done.wait(act, b, K * g + K - 1)
                    filled["xct"].wait_previous(act, b)
                    act.activation(xc[:, g, :], xconv[:, g, :], ACT.Silu).then_inc(xc_ready.sem, 1)
                yield 17
                dt_step.wait(act, b, 1)
                act.activation(dtu[:, :, :], dtv[:, :, :], ACT.Exp).then_inc(dt_exp.sem, 1)
                dt_exp.wait(act, b)
                act.activation(dtl[:, :, :], dtu[:, :, :], ACT.Ln, bias=1.0).then_inc(dt_ln.sem, 1)
                btd_ready.wait(act, b)
                route_step.wait_previous(act, b)
                act.activation(sig[:, :, :], btd[:, :, N + H:], ACT.Exp, scale=-1.0).then_inc(affexp_ready.sem, 1)
                ncum_ready.wait(act, b)
                yint_ready.wait_previous(act, b)
                act.activation(ecum[:, :, :], ncum[:, :, :], ACT.Exp, scale=-1.0).then_inc(ecum_ready.sem, 1)
                for j in range(J):
                    arg_ready.wait(act, b, j)
                    act.activation(decay[:, j, :, :], decay[:, j, :, :], ACT.Exp).then_inc(decay_ready.sem, 1)
                stated_ready.wait_previous(act, b)
                act.activation(cdec[:, :, :], cend[:, :, :], ACT.Exp).then_inc(cdec_ready.sem, 1)
                yield 20
                filled["cwt"].wait(act, b)
                if not first(b):
                    gate_ready.wait_previous(act, b - 1)
                act.activation(at(CW, b), bank_of("cwt")[:, :], ACT.Copy).then_inc(cw_kept.sem, 1)
                cw_kept.wait(act, b)
                act.sem_inc(free_of("cwt"), 1)

                def transposed(j):
                    filled["ygt"].wait(act, b, j)
                    (filled["outp"].wait(act, b, j - 2) if j >= 2 else filled["outp"].wait_previous(act, b, J - 2 + j))
                    act.activation(ygt[:, j % 2, :], bank_of("ygt", j)[:, 0:DI], ACT.Copy).then_inc(ygt_ready.sem, 1)
                    ygt_ready.wait(act, b, j)
                    act.sem_inc(free_of("ygt", j), 1)

                for j in range(J):
                    yield Y_SLOT[j]
                    y_ready.wait(act, b, j)
                    if j:
                        ss_ready.wait(act, b, j - 1)
                    rs_ready.wait_previous(act, b)
                    act.activation(ysq[:, :], y[:, j % 2, :], ACT.Square, accum_out=ss[:, j:j + 1]).then_inc(ss_ready.sem, 1)
                    if j:
                        yield Y_SLOT[j] + 1
                        transposed(j - 1)
                yield Y_SLOT[J - 1] + 2
                transposed(J - 1)

            def experts(b, mixer):
                def high(p):
                    prod_ready.wait(act, b, p)
                    (down_done.wait(act, b, p - 2) if p >= 2 else down_done.wait_previous(act, b, NQ - 2 + p))
                    rows_ = P if p < NP else F
                    act.activation(ph[0:rows_, p % 2, :], prod[0:rows_, p % 2, :], ACT.Copy).then_inc(ph_ready.sem, 1)

                for p in range(NQ):
                    u_filled.wait(act, b, p)
                    (prod_ready.wait(act, b, p - 2) if p >= 2 else prod_ready.wait_previous(act, b, NQ - 2 + p))
                    rows_ = P if p < NP else F
                    if p < NP:
                        act.activation(hid[:, p % 2, :], bank[U_BANK[p % 2]][:, :], ACT.Silu).then_inc(u_read.sem, 1)
                    else:
                        pl_ready.wait(act, b, p - 2)
                        act.activation(prod[0:F, p % 2, :], bank[U_BANK[p % 2]][0:F, :], ACT.Silu).then_inc(u_read.sem, 1)
                    if p:
                        high(p - 1)
                    step(mixer, p)
                high(NP)
                step(mixer, NQ + 1)
                down_done.wait(act, b)
                g_filled.wait_previous(act, b)
                act.activation(gate_t[:, :], bank[Y_BANK][:, :], ACT.Silu).then_inc(gate_ready.sem, 1)

            run(act, front, experts)

        @block.vector
        def _(dve):
            for s in (stats_ready, xn_ready, xl_ready, tap_done, dt_step, ncum_ready, arg_ready, biased_ready,
                      top8_ready, replaced_ready, route_step, smask_ready, xdt_ready, yint_ready, y_ready,
                      state_ready, s_kept, da_step, arg_part, cw_part, prod_ready, pl_ready, fin_step, fin_read, *bank_free):
                s.start(dve)
            for n, (src, hi, lo) in enumerate(SPLITS):
                dve.wait_ge(s_split_hi, n + 1)
                dve.tensor_tensor(lo.rearrange("p a t -> p (a t)"), land[n % 2],
                                  hi.rearrange("p a t -> p (a t)").bitcast(F32), ALU.subtract).then_inc(s_split_lo, 1)
            n = len(SPLITS)
            dve.wait_ge(s_split_hi, n + 1)
            dve.tensor_tensor(wp_lo[:, :], small[:, 0:WP], wp_hi[:, :].bitcast(F32), ALU.subtract).then_inc(s_split_lo, 1)
            dve.wait_ge(s_split_hi, n + 2)
            dve.tensor_tensor(up_lo[:, NP, 0:F], hid[:, 0, 0:F], up_hi[:, NP, 0:F].bitcast(F32), ALU.subtract)\
                .then_inc(s_split_lo, 1)
            dve.wait_ge(s_split_hi, n + 3)
            dve.tensor_tensor(dn_lo[0:F, NP, :], hid[0:F, 1, 0:D], dn_hi[0:F, NP, :].bitcast(F32), ALU.subtract)\
                .then_inc(s_split_lo, 1)
            dve.wait_ge(s_setup, 3)
            dve.tensor_scalar(neg_a[:, :], neg_a[:, :], -1.0, None, ALU.mult).then_inc(s_setup, 1)
            dve.wait_ge(s_setup, 4)
            dve.wait_ge(s_weights[1], 16)

            def front(b):
                yield 0
                dve.wait_ge(x_landed, b * 16 + 16)
                rstd_ready.wait_previous(dve, b)
                for j in range(J):
                    dve.bn_stats(stats[:, j, :], x_tok[:, j, :]).then_inc(stats_ready.sem, 1)
                stats_ready.wait(dve, b, J - 1)
                apart(dve)
                for j in range(J):
                    dve.bn_aggr(mv[:, j, :], stats[:, j, :]).then_inc(stats_ready.sem, 1)
                stats_ready.wait(dve, b)
                yield 1
                rstd_ready.wait(dve, b)
                for j in range(J):
                    dve.tensor_scalar(x_tok[:, j, :], x_tok[:, j, :], mv[:, j, 0:1], rstd[:, j:j + 1],
                                      ALU.subtract, ALU.mult).then_inc(xn_ready.sem, 1)
                yield 4
                xh_ready.wait(dve, b)
                filled["bc"].wait_previous(dve, b)
                if not first(b):
                    kept_x.wait_previous(dve, b)
                dve.tensor_tensor(xl[:, :], bank_of("xnt")[:, :], xh[:, :].bitcast(F32), ALU.subtract).then_inc(xl_ready.sem, 1)
                xl_ready.wait(dve, b)
                dve.sem_inc(free_of("xnt"), 1)

                yield 10
                btd_ready.wait(dve, b)
                dt_exp.wait_previous(dve, b)
                dve.tensor_tensor(dtv[:, :, :], btd[:, :, N:N + H],
                                  rows_sb[:, E:E + H].unsqueeze(1).to_broadcast([P, J, H]), ALU.add).then_inc(dt_step.sem, 1)
                dt_step.wait(dve, b, 0)
                dve.tensor_scalar(dtv[:, :, :], dtv[:, :, :], DT_CAP, None, ALU.min).then_inc(dt_step.sem, 1)

                yield 11
                replaced_ready.wait_previous(dve, b)
                dve.tensor_tensor(biased[:, :, :], btd[:, :, N + H:],
                                  rows_sb[:, 0:E].unsqueeze(1).to_broadcast([P, J, E]), ALU.add).then_inc(biased_ready.sem, 1)
                biased_ready.wait(dve, b)
                apart(dve)
                for j in range(J):
                    dve.max(top8[:, j, :], biased[:, j, :]).then_inc(top8_ready.sem, 1)
                for j in range(J):
                    top8_ready.wait(dve, b, j)
                    apart(dve)
                    dve.match_replace(replaced[:, j, :], top8[:, j, :], biased[:, j, :], LOWEST).then_inc(replaced_ready.sem, 1)

                for g in range(G):
                    yield 12 + 2 * g
                    xraw_ready.wait(dve, b, g)
                    xc_ready.wait_previous(dve, b, g)
                    dve.tensor_scalar(xconv[:, g, :], xraw[:, g, 0:T], conv_sb[:, g, 0:1], None, ALU.mult).then_inc(tap_done.sem, 1)
                    for k in range(1, K):
                        yield 12 + 2 * g + k // 2
                        tap_done.wait(dve, b, K * g + k - 1)
                        dve.scalar_tensor_tensor(xconv[:, g, :], xraw[:, g, k:k + T], conv_sb[:, g, k:k + 1], xconv[:, g, :],
                                                 ALU.mult, ALU.add).then_inc(tap_done.sem, 1)

                yield 17
                dt_exp.wait(dve, b)
                dve.tensor_scalar(dtw[:, :, :], dtu[:, :, :], 1.0, -1.0, ALU.add, ALU.add).then_inc(dt_step.sem, 1)
                dt_step.wait(dve, b, 2)
                dve.tensor_scalar(dtw[:, :, :], dtw[:, :, :], 1e-30, None, ALU.max).then_inc(dt_step.sem, 1)
                dt_step.wait(dve, b, 3)
                dve.reciprocal(dtr[:, :, :], dtw[:, :, :]).then_inc(dt_step.sem, 1)
                dt_ln.wait(dve, b)
                dt_step.wait(dve, b, 4)
                dve.tensor_tensor(dtr[:, :, :], dtr[:, :, :], dtu[:, :, :], ALU.mult).then_inc(dt_step.sem, 1)
                dt_step.wait(dve, b, 5)
                dve.tensor_tensor(dtr[:, :, :], dtr[:, :, :], dtl[:, :, :], ALU.mult).then_inc(dt_step.sem, 1)
                dt_step.wait(dve, b, 6)
                dve.tensor_scalar(dt_[:, :, :], dtr[:, :, :], DT_MIN, DT_MAX, ALU.max, ALU.min).then_inc(dt_step.sem, 1)
                dt_step.wait(dve, b, 7)
                filled["cumb"].wait_previous(dve, b)
                dve.tensor_tensor(da[:, :, :], dt_[:, :, :], neg_a[:, :].unsqueeze(1).to_broadcast([P, J, H]), ALU.mult)\
                    .then_inc(da_step.sem, 1)
                da_step.wait(dve, b, 0)
                dve.tensor_copy(da_hi[:, :, :], da[:, :, :]).then_inc(da_step.sem, 1)
                da_step.wait(dve, b, 1)
                dve.tensor_tensor(da_lo[:, :, :], da[:, :, :], da_hi[:, :, :].bitcast(F32), ALU.subtract).then_inc(da_step.sem, 1)
                dve.sem_inc(dt_step.sem, 1)

                filled["cum"].wait(dve, b)
                ecum_ready.wait_previous(dve, b)
                dve.tensor_scalar(ncum[:, :, :].rearrange("p j h -> p (j h)"), bank_of("cum")[:, 0:J * H], -1.0, None, ALU.mult)\
                    .then_inc(ncum_ready.sem, 1)
                ncum_ready.wait(dve, b)
                dve.sem_inc(free_of("cum"), 1)
                for j in range(J):
                    filled["cumb"].wait(dve, b, j)
                    if j == 0:
                        mix_ready.wait_previous(dve, b)
                        xw_ready.wait_previous(dve, b)
                        cdec_ready.wait_previous(dve, b)
                    ps = bank_of("cumb", j)[:, :].rearrange("p (h t) -> p h t", h=H)
                    for h in range(H):
                        dve.tensor_scalar(decay[:, j, h, :], ps[:, h, :], ncum[:, j, h:h + 1], 0.0, ALU.add, ALU.min)\
                            .then_inc(arg_part.sem, 1)
                    dve.tensor_copy(cend[:, j, :], ps[:, :, P - 1]).then_inc(arg_part.sem, 1)
                    arg_part.wait(dve, b, (H + 1) * (j + 1) - 1)
                    dve.sem_inc(arg_ready.sem, 1)
                    dve.sem_inc(free_of("cumb", j), 1)

                yield 18
                replaced_ready.wait(dve, b)
                dve.tensor_tensor(replaced[:, :, :], replaced[:, :, :], biased[:, :, :], ALU.not_equal).then_inc(route_step.sem, 1)
                affexp_ready.wait(dve, b)
                dve.tensor_scalar(sig[:, :, :], sig[:, :, :], 1.0, None, ALU.add).then_inc(route_step.sem, 1)
                route_step.wait(dve, b, 1)
                dve.reciprocal(sig[:, :, :], sig[:, :, :]).then_inc(route_step.sem, 1)
                route_step.wait(dve, b, 2)
                dve.tensor_tensor(sig[:, :, :], sig[:, :, :], replaced[:, :, :], ALU.mult).then_inc(route_step.sem, 1)
                route_step.wait(dve, b, 3)
                dve.tensor_reduce(wsum[:, :], sig[:, :, :], AX_X, ALU.add).then_inc(route_step.sem, 1)
                route_step.wait(dve, b, 4)
                dve.tensor_scalar(wsum[:, :], wsum[:, :], 1e-8, None, ALU.add).then_inc(route_step.sem, 1)
                route_step.wait(dve, b, 5)
                dve.reciprocal(wrec[:, :], wsum[:, :]).then_inc(route_step.sem, 1)
                route_step.wait(dve, b, 6)
                dve.tensor_tensor(sig[:, :, :], sig[:, :, :], wrec[:, :].unsqueeze(2).to_broadcast([P, J, E]), ALU.mult)\
                    .then_inc(route_step.sem, 1)
                route_step.wait(dve, b, 7)
                filled["cwt"].wait_previous(dve, b)
                dve.tensor_copy(cw_cat[:, :, 0, :].bitcast(F32R), sig[:, :, :]).then_inc(cw_part.sem, 1)
                cw_part.wait(dve, b, 0)
                dve.tensor_tensor(cw_cat[:, :, 1, :], sig[:, :, :], cw_cat[:, :, 0, :], ALU.subtract).then_inc(cw_part.sem, 1)
                cw_part.wait(dve, b, 1)
                dve.sem_inc(route_step.sem, 1)

                def chunk_inputs(j):
                    q = j % 2
                    filled["xct"].wait(dve, b, j)
                    (filled["y"].wait(dve, b, j - 2) if j >= 2 else filled["y"].wait_previous(dve, b, J - 2 + j))
                    (xw_ready.wait(dve, b, j - 2) if j >= 2 else xw_ready.wait_previous(dve, b, J - 2 + j))
                    dve.tensor_tensor(xdt[:, q, :].rearrange("p (h n) -> p h n", h=H),
                                      bank_of("xct", j)[:, 0:DI].rearrange("p (h n) -> p h n", h=H),
                                      dt_[:, j, :].unsqueeze(2).to_broadcast([P, H, HP]), ALU.mult).then_inc(xdt_ready.sem, 1)
                    xdt_ready.wait(dve, b, j)
                    dve.sem_inc(free_of("xct", j), 1)
                    filled["score"].wait(dve, b, j)
                    (mix_ready.wait(dve, b, j - 2) if j >= 2 else mix_ready.wait_previous(dve, b, J - 2 + j))
                    dve.tensor_tensor(smask[:, q, :], bank_of("score", j)[:, 0:P], upper[:, :], ALU.mult).then_inc(smask_ready.sem, 1)
                    smask_ready.wait(dve, b, j)
                    dve.sem_inc(free_of("score", j), 1)

                def output(j):
                    filled["outp"].wait(dve, b, j)
                    rs_ready.wait(dve, b, 2 * j + 1)
                    dve.tensor_scalar(at(S, b)[:, j * D:(j + 1) * D], bank_of("outp", j)[:, 0:D], rs[:, j:j + 1], None, ALU.mult)\
                        .then_inc(s_kept.sem, 1)
                    s_kept.wait(dve, b, j)
                    dve.sem_inc(free_of("outp", j), 1)

                for j in range(2):
                    yield 20 + j
                    chunk_inputs(j)
                for j in range(J):
                    q = j % 2
                    yield Y_SLOT[j]
                    filled["y"].wait(dve, b, j)
                    ps = bank_of("y", j)
                    if j >= 2:
                        yg_ready.wait(dve, b, j - 2)
                        ss_ready.wait(dve, b, j - 2)
                    else:
                        yg_ready.wait_previous(dve, b, J - 2 + j)
                        ss_ready.wait_previous(dve, b, J - 2 + j)
                    if j:
                        ecum_ready.wait(dve, b)
                        dve.tensor_tensor(yint[:, q, :].rearrange("p (h n) -> p h n", h=H),
                                          ps[:, DI:2 * DI].rearrange("p (h n) -> p h n", h=H),
                                          ecum[:, j, :].unsqueeze(2).to_broadcast([P, H, HP]), ALU.mult).then_inc(yint_ready.sem, 1)
                        yint_ready.wait(dve, b, j)
                        dve.tensor_tensor(y[:, q, :], ps[:, 0:DI], yint[:, q, :], ALU.add).then_inc(y_ready.sem, 1)
                    else:
                        dve.sem_inc(yint_ready.sem, 1)
                        dve.tensor_copy(y[:, q, :], ps[:, 0:DI]).then_inc(y_ready.sem, 1)
                    y_ready.wait(dve, b, j)
                    dve.sem_inc(free_of("y", j), 1)
                    if j + 1 < J:
                        filled["delta"].wait(dve, b, j)
                        if j == 0:
                            filled["y"].wait_previous(dve, b)
                            stated_ready.wait_previous(dve, b)
                            dve.tensor_copy(state[:, 0, :], bank_of("delta", j)[0:N, 0:DI]).then_inc(state_ready.sem, 1)
                        else:
                            stated_ready.wait(dve, b, j - 1)
                            dve.tensor_tensor(state[:, j, :], bank_of("delta", j)[0:N, 0:DI], state_d[:, j - 1, :], ALU.add)\
                                .then_inc(state_ready.sem, 1)
                        state_ready.wait(dve, b, j)
                        dve.sem_inc(free_of("delta", j), 1)
                    if j:
                        yield Y_SLOT[j] + 1
                        output(j - 1)
                    if j + 2 < J:
                        yield Y_SLOT[j] + 2
                        chunk_inputs(j + 2)
                yield Y_SLOT[J - 1] + 2
                output(J - 1)
                dve.sem_inc(state_ready.sem, 1)

            def experts(b, mixer):
                def low(p):
                    ph_ready.wait(dve, b, p)
                    n = P if p < NP else F
                    (down_done.wait(dve, b, p - 2) if p >= 2 else down_done.wait_previous(dve, b, NQ - 2 + p))
                    dve.tensor_tensor(pl[0:n, p % 2, :], prod[0:n, p % 2, :], ph[0:n, p % 2, :].bitcast(F32), ALU.subtract)\
                        .then_inc(pl_ready.sem, 1)

                for p in range(NP):
                    u_read.wait(dve, b, p)
                    c_filled.wait(dve, b, p)
                    (pl_ready.wait(dve, b, p - 2) if p >= 2 else pl_ready.wait_previous(dve, b, NQ - 2 + p))
                    dve.tensor_tensor(prod[:, p % 2, :], hid[:, p % 2, :], bank[C_BANK[p % 2]][:, :], ALU.mult)\
                        .then_inc(prod_ready.sem, 1)
                    if p:
                        low(p - 1)
                    step(mixer, p)
                u_read.wait(dve, b, NP)
                dve.sem_inc(prod_ready.sem, 1)
                low(NP - 1)
                low(NP)
                step(mixer, NQ + 1)
                g_filled.wait(dve, b)
                fin_read.wait_previous(dve, b)
                dve.tensor_tensor(fin[:, :, :].rearrange("p j d -> p (j d)"), at(S, b), bank[Y_BANK][:, :], ALU.mult)\
                    .then_inc(fin_step.sem, 1)
                fin_step.wait(dve, b, 0)
                dve.wait_ge(xres_landed, b * 16 + 16)
                dve.tensor_tensor(fin[:, :, :], fin[:, :, :], x_res[:, :, :], ALU.add).then_inc(fin_step.sem, 1)

            run(dve, front, experts)

        @block.tensor
        def _(pe):
            for s in (*filled.values(), u_filled, c_filled, down_done, g_filled):
                s.start(pe)

            def mm3(out_, lhs_hi, lhs_lo, rhs_hi, rhs_lo, start=True, stop=True):
                pe.matmul(out_, lhs_hi, rhs_lo, start=start, stop=False)
                pe.matmul(out_, lhs_lo, rhs_hi, start=False, stop=False)
                return pe.matmul(out_, lhs_hi, rhs_hi, start=False, stop=stop)

            pe.wait_ge(s_split_lo, len(SPLITS) + 3)
            pe.wait_ge(s_setup, 4)
            pe.wait_ge(s_const, 9)
            pe.wait_ge(s_weights[2], 16)

            def front(b):
                yield 2
                wait_bank(pe, b, "xnt")
                for j in range(J):
                    xn_ready.wait(pe, b, j)
                    last = pe.transpose(bank_of("xnt")[:, j * P:(j + 1) * P], x_tok[:, j, :], ident[:, :])
                last.then_inc(filled["xnt"].sem, 1)
                for j in range(J):
                    yield 6 + j
                    xh_ready.wait(pe, b)
                    xl_ready.wait(pe, b)
                    wait_bank(pe, b, "tok", j)
                    t = slice(j * P, (j + 1) * P)
                    mm3(bank_of("tok", j)[:, 0:TOK], xh[:, t], xl[:, t], wp_hi[:, 0:TOK], wp_lo[:, 0:TOK])\
                        .then_inc(filled["tok"].sem, 1)
                for g in range(G):
                    yield 10 + g
                    wait_bank(pe, b, "conv", g)
                    c = slice(C_CONV + g * P, C_CONV + (g + 1) * P)
                    mm3(bank_of("conv", g)[:, :], wp_hi[:, c], wp_lo[:, c], xh[:, :], xl[:, :]).then_inc(filled["conv"].sem, 1)
                yield 12
                wait_bank(pe, b, "bc")
                c = slice(C_BC, C_BC + 2 * N)
                mm3(bank_of("bc")[:, :], wp_hi[:, c], wp_lo[:, c], xh[:, :], xl[:, :]).then_inc(filled["bc"].sem, 1)

                yield 17
                wait_bank(pe, b, "cum")
                da_step.wait(pe, b)
                pe.matmul(bank_of("cum")[:, 0:J * H], upper[:, :], da[:, :, :].rearrange("p j h -> p (j h)"),
                          start=True, stop=True).then_inc(filled["cum"].sem, 1)
                for j in range(J):
                    wait_bank(pe, b, "cumb", j)
                    for h in range(H):
                        o = bank_of("cumb", j)[:, h * P:(h + 1) * P]
                        pe.matmul(o, da_hi[:, j, h:h + 1].to_broadcast([P, P]), upper_r[:, :], start=True, stop=False)
                        last = pe.matmul(o, da_lo[:, j, h:h + 1].to_broadcast([P, P]), upper_r[:, :], start=False, stop=True)
                    last.then_inc(filled["cumb"].sem, 1)
                yield 19
                wait_bank(pe, b, "cwt")
                cw_part.wait(pe, b)
                for j in range(J):
                    last = pe.transpose(bank_of("cwt")[:, j * P:(j + 1) * P],
                                        cw_cat[:, j, :, :].rearrange("p a e -> p (a e)"), ident[:, :])
                last.then_inc(filled["cwt"].sem, 1)

                def chunk_inputs(j):
                    t = slice(j * P, (j + 1) * P)
                    wait_bank(pe, b, "xct", j)
                    for g in range(G):
                        xc_ready.wait(pe, b, g)
                        last = pe.transpose(bank_of("xct", j)[:, g * P:(g + 1) * P], xc[:, g, t], ident[:, :])
                    last.then_inc(filled["xct"].sem, 1)
                    wait_bank(pe, b, "score", j)
                    bt_ready.wait(pe, b)
                    ct_ready.wait(pe, b)
                    pe.matmul(bank_of("score", j)[:, 0:P], bt[:, t], ct[:, t], start=True, stop=True)\
                        .then_inc(filled["score"].sem, 1)

                def output(j):
                    q = j % 2
                    wait_bank(pe, b, "ygt", j)
                    yg_ready.wait(pe, b, j)
                    for g in range(G):
                        last = pe.transpose(bank_of("ygt", j)[:, g * P:(g + 1) * P], yg[:, q, g * P:(g + 1) * P], ident[:, :])
                    last.then_inc(filled["ygt"].sem, 1)
                    wait_bank(pe, b, "outp", j)
                    ygt_ready.wait(pe, b, j)
                    for g in range(G):
                        last = pe.matmul(bank_of("outp", j)[:, 0:D], ygt[:, q, g * P:(g + 1) * P], w_out_sb[:, g, :],
                                         start=(g == 0), stop=(g == G - 1))
                    last.then_inc(filled["outp"].sem, 1)

                for j in range(2):
                    yield 20 + j
                    chunk_inputs(j)
                for j in range(J):
                    q = j % 2
                    t = slice(j * P, (j + 1) * P)
                    yield Y_SLOT[j]
                    wait_bank(pe, b, "y", j)
                    xdt_ready.wait(pe, b, j)
                    mix_ready.wait(pe, b, j)
                    ps = bank_of("y", j)
                    for h in range(H):
                        last = pe.matmul(ps[:, h * HP:(h + 1) * HP], mix[:, q, h, :], xdt[:, q, h * HP:(h + 1) * HP],
                                         start=True, stop=True)
                    if j:
                        state_ready.wait(pe, b, j - 1)
                        last = pe.matmul(ps[:, DI:2 * DI], ct[:, t], state[:, j - 1, :], start=True, stop=True)
                    last.then_inc(filled["y"].sem, 1)
                    if j + 1 < J:
                        wait_bank(pe, b, "delta", j)
                        xw_ready.wait(pe, b, j)
                        pe.matmul(bank_of("delta", j)[0:N, 0:DI], btd[:, j, 0:N], xw[:, q, :], start=True, stop=True)\
                            .then_inc(filled["delta"].sem, 1)
                    if j:
                        yield Y_SLOT[j] + 1
                        output(j - 1)
                    if j + 2 < J:
                        yield Y_SLOT[j] + 2
                        chunk_inputs(j + 2)
                yield Y_SLOT[J - 1] + 2
                output(J - 1)

            def experts(b, mixer):
                def up(p):
                    (u_read.wait(pe, b, p - 2) if p >= 2 else u_read.wait_previous(pe, b, NQ - 2 + p))
                    n = P if p < NP else F
                    if p == NP:
                        apart(pe)
                    mm3(bank[U_BANK[p % 2]][0:n, :], up_hi[:, p, 0:n], up_lo[:, p, 0:n], at(XH, b), at(XL, b))\
                        .then_inc(u_filled.sem, 1)
                    if p < NP:
                        (prod_ready.wait(pe, b, p - 2) if p >= 2 else prod_ready.wait_previous(pe, b, NP - 2 + p))
                        pe.matmul(bank[C_BANK[p % 2]][:, :], stair[:, 2 * p:2 * p + 2, :].rearrange("p e f -> p (e f)"),
                                  at(CW, b), start=True, stop=True).then_inc(c_filled.sem, 1)

                def down(p):
                    ph_ready.wait(pe, b, p)
                    pl_ready.wait(pe, b, p)
                    if p == 0:
                        fin_step.wait_previous(pe, b, 0)
                    n = P if p < NP else F
                    mm3(bank[Y_BANK][:, :], dn_hi[0:n, p, :], dn_lo[0:n, p, :], ph[0:n, p % 2, :], pl[0:n, p % 2, :],
                        start=(p == 0), stop=(p == NP)).then_inc(down_done.sem, 1)

                kept_x.wait(pe, b)
                cw_kept.wait(pe, b)
                up(0)
                up(1)
                for p in range(NQ + 2):
                    if p + 2 < NQ:
                        up(p + 2)
                    if p >= 2:
                        down(p - 2)
                    step(mixer, p)
                gate_ready.wait(pe, b)
                for j in range(J):
                    last = pe.transpose(bank[Y_BANK][:, j * P:(j + 1) * P], gate_t[:, j * P:(j + 1) * P], ident[:, :])
                last.then_inc(g_filled.sem, 1)

            run(pe, front, experts)


def kernel(**inputs):
    import numpy as np
    import concourse.bacc as bacc
    from concourse.bass_utils import run_bass_kernel_spmd

    a = {k: np.asarray(v) for k, v in inputs.items()}
    w_in = a["L0_attn_W_in"].T
    w_out = a["L0_attn_W_out"].T
    cent = a["L0_ffn_centroids"].T
    D, DI = w_in.shape[0], w_out.shape[0]
    E, _, F = a["L0_ffn_W_up"].shape
    H = a["L0_attn_A_log"].shape[0]
    N = (w_in.shape[1] - 2 * DI - H) // 2
    z, xc, B, C, dt = np.split(w_in, [DI, 2 * DI, 2 * DI + N, 2 * DI + 2 * N], axis=1)
    row = np.concatenate([a["L0_ffn_expert_biases"], a["L0_attn_dt_bias"], a["L0_attn_A_log"]])
    arrays = {
        "x": a["L0_attn_x"],
        "w_proj": np.concatenate([z, B, dt, cent, xc, B, C], axis=1),
        "w_out_t": w_out.reshape(DI // 128, 128, D).transpose(1, 0, 2),
        "conv_w": a["L0_attn_conv_w"].reshape(DI // 128, 128, -1).transpose(1, 0, 2),
        "rows": np.broadcast_to(row, (128, row.size)),
        "w_up": a["L0_ffn_W_up"].transpose(1, 0, 2).reshape(D, E * F),
        "w_down": a["L0_ffn_W_down"].reshape(E // 2, 2 * F, D).transpose(1, 0, 2).reshape(2 * F, (E // 2) * D),
        "ws_up": a["L0_ffn_Ws_up"],
        "ws_down": a["L0_ffn_Ws_down"],
    }
    arrays = {k: np.ascontiguousarray(v) for k, v in arrays.items()}
    nc = bacc.Bacc("TRN2", target_bir_lowering=False, num_devices=1)
    args = [nc.dram_tensor(k, v.shape, F32, kind="ExternalInput").ap() for k, v in arrays.items()]
    out = nc.dram_tensor("out", a["L0_attn_x"].shape, F32, kind="ExternalOutput").ap()
    build(nc, *args, out)
    r = run_bass_kernel_spmd(nc, [arrays], core_ids=[0])
    return r.results[0]["out"]
```

```python
from contextlib import ExitStack

import concourse.bass as bass
from concourse import mybir

F32 = mybir.dt.float32
F32R = mybir.dt.float32r
ALU = mybir.AluOpType
ACT = mybir.ActivationFunctionType
AX_X = mybir.AxisListType.X

P = 128
LOWEST = -3.4028234e38
LN_EPS = 1e-5
RMS_EPS = 1.1920929e-07
DT_CAP = 20.0
DT_MIN, DT_MAX = 1e-4, 0.5
RING = 3
DEPTH = 3


class Signal:

    def __init__(self, sem, per):
        self.sem, self.per = sem, per

    def start(self, eng):
        eng.sem_inc(self.sem, self.per)

    def wait(self, eng, b, k=None):
        k = self.per - 1 if k is None else k
        eng.wait_ge(self.sem, b * self.per + (self.per + k + 1))

    def wait_previous(self, eng, b, k=None):
        k = self.per - 1 if k is None else k
        eng.wait_ge(self.sem, b * self.per + (k + 1))


def build(nc, x, w_proj, w_out_t, conv_w, rows, w_up, w_down, ws_up, ws_down, out):
    NB, T, D = x.shape
    J = T // P
    E = rows.shape[1] - 8
    H = 4
    DI = 2 * D
    HP = DI // H
    N = (w_proj.shape[1] - 2 * DI - H - E) // 3
    F = ws_up.shape[1]
    NP = E // 2
    G = DI // P
    K = 4
    C_SCALE = float(N) ** -0.5
    TOK = DI + N + H + E
    BTD = N + H + E
    assert D == P and HP * H == DI and 2 * F == P and N == 64

    ctx = ExitStack()
    with ctx:
        def sb(name, shape, dt=F32):
            return ctx.enter_context(nc.sbuf_tensor(name, shape, dt))

        def sem(name):
            return ctx.enter_context(nc.semaphore(name))

        def signal(name, per):
            return Signal(sem(name), per)

        up_hi, up_lo = sb("up_hi", [P, NP + 1, P], F32R), sb("up_lo", [P, NP + 1, P], F32R)
        dn_hi, dn_lo = sb("dn_hi", [P, NP + 1, D], F32R), sb("dn_lo", [P, NP + 1, D], F32R)
        wp_hi, wp_lo = sb("wp_hi", [P, w_proj.shape[1]], F32R), sb("wp_lo", [P, w_proj.shape[1]], F32R)
        w_out_sb = sb("w_out_sb", [P, G, D])
        conv_sb = sb("conv_sb", [P, G, K])
        rows_sb = sb("rows_sb", [P, E + 8])
        neg_a = sb("neg_a", [P, H])
        ident = sb("ident", [P, P])
        upper = sb("upper", [P, P])
        ones = sb("ones", [P, P])
        later = sb("later", [P, P], F32R)
        stair = sb("stair", [P, E, F], F32R)
        minus_half = sb("minus_half", [P, J])
        XH, XL = sb("XH", [P, 2, T], F32R), sb("XL", [P, 2, T], F32R)
        CW = sb("CW", [P, 2, T], F32R)
        S = sb("S", [P, J * D])
        x_tok = sb("x_tok", [P, J, D])
        stats = sb("stats", [P, J, 6])
        mv = sb("mv", [P, J, 2])
        var_e = sb("var_e", [P, J])
        rstd = sb("rstd", [P, J])
        xh, xl = sb("xh", [P, T], F32R), sb("xl", [P, T], F32R)
        sz = sb("sz", [P, J, DI])
        btd = sb("btd", [P, J, BTD])
        xraw = sb("xraw", [P, G, T + K - 1])
        xc = sb("xc", [P, G, T])
        bt, ct = sb("bt", [N, T]), sb("ct", [N, T])
        dtv = sb("dtv", [P, J, H])
        dtu, dtl, dtw = sb("dtu", [P, J, H]), sb("dtl", [P, J, H]), sb("dtw", [P, J, H])
        dtr, dt_ = sb("dtr", [P, J, H]), sb("dt_", [P, J, H])
        da = sb("da", [P, J, H])
        da_hi, da_lo = sb("da_hi", [P, J, H], F32R), sb("da_lo", [P, J, H], F32R)
        spread_hi, spread_lo = sb("spread_hi", [P, 2, H, P], F32R), sb("spread_lo", [P, 2, H, P], F32R)
        grown = sb("grown", [P, 2, J, H])
        decay = sb("decay", [P, J, H, P])
        biased, top8, replaced = sb("biased", [P, J, E]), sb("top8", [P, J, 8]), sb("replaced", [P, J, E])
        sig = sb("sig", [P, J, E])
        wsum, wrec = sb("wsum", [P, J]), sb("wrec", [P, J])
        cw_cat = sb("cw_cat", [P, J, 2, E])
        smask = sb("smask", [P, 2, P])
        mix = sb("mix", [P, 2, H, P])
        xdt, xw = sb("xdt", [P, 2, DI]), sb("xw", [P, 2, DI])
        yint, y = sb("yint", [P, 2, DI]), sb("y", [P, 2, DI])
        ysq, ss, rs = sb("ysq", [P, DI]), sb("ss", [P, J]), sb("rs", [P, J])
        sse = sb("sse", [P, J])
        yg = sb("yg", [P, 2, DI])
        ygt = sb("ygt", [P, 2, DI])
        state, state_d = sb("state", [N, J - 1, DI]), sb("state_d", [N, J - 2, DI])
        hid, prod = sb("hid", [P, DEPTH, T]), sb("prod", [P, DEPTH, T])
        ph, pl = sb("ph", [P, DEPTH, T], F32R), sb("pl", [P, DEPTH, T], F32R)
        gate_t = sb("gate_t", [P, T])
        x_res = sb("x_res", [P, J, D])
        fin = sb("fin", [P, J, D])

        bank = [ctx.enter_context(nc.psum_tensor(f"bank{i}", [P, 512], F32)) for i in range(8)]
        U_BANK, C_BANK, Y_BANK = (3, 4), (5, 6), 7

        SCAN = [("conv", g) for g in range(G)] + [("bc", 0), ("cum", 0)] + [("between", j) for j in range(J)]
        SCAN += [("xct", 0), ("score", 0), ("xct", 1), ("score", 1)]
        for j in range(J):
            SCAN += [("y", j)]
            if j + 1 < J:
                SCAN += [("delta", j)]
            if j:
                SCAN += [("ygt", j - 1), ("outp", j - 1)]
            if j + 2 < J:
                SCAN += [("xct", j + 2), ("score", j + 2)]
        SCAN += [("ygt", J - 1), ("outp", J - 1)]
        ENTER = [("xnt", 0)] + [("tok", j) for j in range(J)] + [("cwt", 0)]
        SLOT = {"conv": [1, 1], "bc": [2], "cum": [2], "between": [2, 3, 4, 4], "xct": [9, 10, 14, 19],
                "score": [9, 11, 15, 19], "y": [13, 16, 19, 22], "delta": [13, 16, 19], "ygt": [17, 19, 22, 25],
                "outp": [19, 22, 24, 28], "xnt": [16], "tok": [20, 21, 21, 23], "cwt": [32]}
        DOWN_SLOT = [3, 3, 3, 4, 5, 7, 9, 10, 11, 12, 12, 13, 15, 15, 16, 18, 19, 20, 21, 22, 23, 24, 25, 26, 27, 28, 29, 30, 31, 32, 33, 34, 35]
        WHEN = {"taps": [2, 3, 4, 2, 4, 5], "xc": [6, 7], "spread": [0, 1, 3, 4], "decay": [6], "stats": [13],
                "xn": [15], "xl": [17], "keep": [19], "dt": [24], "dt_exp": [25], "dt_rest": [25], "route": [26, 26],
                "sigmoid": [25, 28, 26, 27, 27, 28, 29, 29], "dt_ln": [25]}

        def slot_of(fill):
            return SLOT[fill[0]][fill[1]]

        assert SCAN == sorted(SCAN, key=slot_of) and ENTER == sorted(ENTER, key=slot_of)
        FILLS = sorted(SCAN + ENTER, key=slot_of)
        place = {f: n for n, f in enumerate(FILLS)}
        per = {}
        for name, _ in FILLS:
            per[name] = per.get(name, 0) + 1
        filled = {name: signal(f"{name}_in_psum", n) for name, n in per.items()}

        def bank_of(name, k=0):
            return bank[place[name, k] % RING]

        def wait_bank(pe, b, name, k=0, alone=False):
            part = ENTER if (name, k) in ENTER else SCAN
            n = place[name, k] - RING
            while alone and n >= 0 and FILLS[n] not in part:
                n -= RING
            if alone and n < 0 and part is ENTER:
                return
            turn = 0
            if n < 0:
                turn = -1
                n = max(m for m in range(len(FILLS)) if (m - place[name, k]) % RING == 0)
            before, i = FILLS[n]
            apart_by = turn + (FILLS[n] in ENTER) - ((name, k) in ENTER)
            assert apart_by >= -1
            if apart_by < 0:
                readers[before].wait_previous(pe, b, i)
            else:
                readers[before].wait(pe, b + apart_by if apart_by else b, i)

        s_weights = [sem(f"weights_{i}_landed") for i in range(8)]
        s_piece = [sem(f"expert_weights_{i}_landed") for i in range(5)]
        s_const = sem("constants_made")
        s_split_hi, s_split_lo = sem("weight_high_parts_made"), sem("weight_low_parts_made")
        s_setup = sem("setup_made")
        s_stair = sem("stairs_made")
        s_passed = sem("lone_waits_passed")
        x_landed = sem("x_landed")
        stats_ready = signal("stats_ready", 2 * J)
        var_ready, rstd_ready = signal("var_ready", 1), signal("rstd_ready", 1)
        xn_ready = signal("xn_ready", J)
        xh_ready, xl_ready = signal("xh_ready", 1), signal("xl_ready", 1)
        kept_x = signal("xh_xl_kept", 2)
        sz_ready, btd_ready = signal("silu_z_ready", J), signal("btd_ready", J)
        xraw_ready = signal("xraw_ready", G)
        bt_ready, ct_ready = signal("bt_ready", 1), signal("ct_ready", 1)
        tap_done = [signal(f"conv_{g}_tap_done", K - 1) for g in range(G)]
        tap0_done = signal("first_taps_done", G)
        xc_ready = signal("xc_ready", G)
        dt_step, dt_exp, dt_ln = signal("dt_step_done", 9), signal("dt_exp_ready", 1), signal("dt_ln_ready", 1)
        spread_ready = signal("spread_ready", 2 * J)
        grown_ready, decay_ready = signal("decay_from_start_ready", 1), signal("decay_ready", J)
        da_step, cw_part = signal("da_step_done", 3), signal("cw_part_done", 2)
        biased_ready, top8_ready, replaced_ready = signal("biased_ready", 1), signal("top8_ready", J), signal("replaced_ready", J)
        affexp_ready, route_step = signal("affinity_exp_ready", 1), signal("route_step_done", J + 8)
        cw_kept = signal("cw_kept", 1)
        smask_ready, mix_ready = signal("masked_scores_ready", J), signal("mix_ready", J)
        xdt_ready, xw_ready = signal("xdt_ready", J), signal("xw_ready", J)
        yint_ready, y_ready = signal("y_inter_ready", J), signal("y_ready", J)
        ss_ready, rs_ready = signal("y_square_sum_ready", J), signal("y_rstd_ready", 2 * J)
        yg_ready, ygt_ready = signal("gated_y_ready", J), signal("gated_y_t_ready", J)
        stated_ready, state_ready = signal("state_decayed", J), signal("state_ready", J)
        s_kept = signal("s_kept", J)
        readers = {"xnt": xl_ready, "tok": btd_ready, "conv": xraw_ready, "bc": ct_ready, "cum": grown_ready,
                   "between": decay_ready, "cwt": cw_kept, "xct": xdt_ready, "score": smask_ready, "y": y_ready,
                   "delta": state_ready, "ygt": ygt_ready, "outp": s_kept}
        NQ = NP + 1
        u_filled, u_read = signal("up_in_psum", NQ), signal("hidden_ready", NQ)
        c_filled = signal("weights_in_psum", NP)
        prod_ready = signal("weighted_hidden_ready", NP)
        ph_ready = signal("high_part_ready", NQ)
        POOL_LOWS = [0, 3, 4, 6, 7, 9, 11, 13, 16, 19, 23, 24, 25, 26, 27, 28, 30]
        low_of = [("pool", POOL_LOWS.index(p)) if p in POOL_LOWS else ("dve", p - sum(q < p for q in POOL_LOWS)) for p in range(NQ)]
        low_ready = {"pool": signal("low_part_from_pool_ready", len(POOL_LOWS)),
                     "dve": signal("low_part_from_dve_ready", NQ - len(POOL_LOWS))}
        down_done = signal("down_product_done", NQ)
        gate_ready = signal("gate_t_ready", 1)
        g_filled = signal("gate_in_psum", 1)
        fin_step, fin_read = signal("result_step_done", 2), signal("result_stored", 1)
        xres_landed = sem("x_residual_landed")
        stored = sem("result_landed_in_dram")

        block = ctx.enter_context(nc.Block())

        def at(tile, b):
            return tile[:, bass.ds(b % 2, 1), :].rearrange("p a t -> p (a t)")

        def apart(eng):
            eng.sem_inc(s_passed, 1)

        CONSTANTS = 7
        SPLIT_SLOT = [15, 18, 21, 24, 24, 25, 27, 29]


        def merge(*parts):
            parts = [[next(part), part] for part in parts]
            while parts:
                head = min(parts, key=lambda part: part[0])
                yield head[0]
                head[0] = next(head[1], None)
                if head[0] is None:
                    parts.remove(head)

        class Mixer:

            def __init__(self, steps):
                self.steps, self.slot = steps, next(steps)

            def advance(self, p):
                while self.slot <= p:
                    self.slot = next(self.steps, LAST + 1)

        def run(steps):
            for _ in steps:
                pass

        LAST = 10 ** 5

        def after(signal_, eng, b, k):
            if k >= 0:
                signal_.wait(eng, b, k)
            else:
                signal_.wait_previous(eng, b)

        def after_low(eng, b, p):
            who, k = low_of[p % NQ]
            (low_ready[who].wait if p >= 0 else low_ready[who].wait_previous)(eng, b, k)

        def take_low(eng, b, p):
            n = P if p < NP else F
            ph_ready.wait(eng, b, p)
            after(down_done, eng, b, p - DEPTH)
            eng.tensor_tensor(pl[0:n, p % DEPTH, :], prod[0:n, p % DEPTH, :], ph[0:n, p % DEPTH, :].bitcast(F32),
                              ALU.subtract).then_inc(low_ready[low_of[p][0]].sem, 1)

        def first(b):
            return isinstance(b, int) and b == 0

        x_view = x.rearrange("b (j p) d -> b p j d", p=P)
        out_view = out.rearrange("b (j p) d -> b p j d", p=P)

        def dram_at(view, b):
            return view[bass.ds(b, 1), :, :, :].rearrange("a p j d -> (a p) j d")

        C_CONV, C_BC = TOK, TOK + DI
        WP = w_proj.shape[1]
        QUARTER = NP // 4

        land = [hid[:, 0:2, :].rearrange("p a t -> p (a t)"), prod[:, 0:2, :].rearrange("p a t -> p (a t)"),
                decay[:, 0:2, :, :].rearrange("p j h t -> p (j h t)"), decay[:, 2:4, :, :].rearrange("p j h t -> p (j h t)"),
                xc[:, :, :].rearrange("p g t -> p (g t)")]
        LANDS = len(land)
        land_proj = mix[:, :, :, :].rearrange("p a h t -> p (a h t)")[:, 0:WP]
        land_su, land_sd = gate_t[:, 0:F], gate_t[0:F, P:P + D]
        SPLITS = []
        for dram, hi, lo in ((w_up, up_hi, up_lo), (w_down, dn_hi, dn_lo)):
            for q in range(0, NP, QUARTER):
                SPLITS.append((dram[:, q * P:(q + QUARTER) * P], hi[:, q:q + QUARTER, :].rearrange("p a t -> p (a t)"),
                               lo[:, q:q + QUARTER, :].rearrange("p a t -> p (a t)")))

        @block.sync
        def _(sp):
            def load(b):
                filled["xnt"].wait_previous(sp, b)
                sp.dma_start(x_tok[:, :, :], dram_at(x_view, b)).then_inc(x_landed, 16)

            def finish(b):
                fin_step.wait_previous(sp, b)
                sp.dma_start(x_res[:, :, :], dram_at(x_view, b)).then_inc(xres_landed, 16)
                fin_step.wait(sp, b)
                sp.dma_start(dram_at(out_view, b), fin[:, :, :]).then_inc(stored, 16)
                sp.wait_ge(stored, b * 16 + 16)
                sp.sem_inc(fin_read.sem, 1)

            load(0)
            sp.dma_start(land_proj, w_proj).then_inc(s_weights[7], 16)
            for n, (src, hi, lo) in enumerate(SPLITS):
                if n >= LANDS:
                    sp.wait_ge(s_split_lo, n - LANDS + 1 + 3)
                sp.dma_start(land[n % LANDS], src).then_inc(s_piece[n % LANDS], 16)
            load(1)
            with sp.Fori(0, NB - 2) as b:
                load(b + 2)
                finish(b)
            finish(NB - 2)
            finish(NB - 1)

        @block.gpsimd
        def _(pool):
            for s in (var_ready, rstd_ready, kept_x, xw_ready, mix_ready, yg_ready, rs_ready, stated_ready,
                      spread_ready, low_ready["pool"]):
                s.start(pool)
            pool.memset(ident[:, :], 0.0).then_inc(s_const, 1)
            pool.memset(upper[:, :], 1.0).then_inc(s_const, 1)
            pool.memset(ones[:, :], 1.0).then_inc(s_const, 1)
            pool.memset(minus_half[:, :], -0.5).then_inc(s_const, 1)
            pool.memset(xraw[:, :, 0:K - 1], 0.0).then_inc(s_const, 1)
            pool.wait_ge(s_const, 5)
            pool.affine_select(out=ident[:, :], in_=ident[:, :], compare_op=ALU.not_equal, fill=1.0, base=0,
                               pattern=[[-1, P]], channel_multiplier=1).then_inc(s_const, 1)
            pool.affine_select(out=upper[:, :], in_=upper[:, :], compare_op=ALU.is_ge, fill=0.0, base=0,
                               pattern=[[1, P]], channel_multiplier=-1).then_inc(s_const, 1)

            def make_stairs():
                flat = stair[:, :, :].rearrange("p e f -> p (e f)")
                pool.memset(flat.bitcast(F32), 0.0).then_inc(s_stair, 1)
                for n in range(2):
                    pool.wait_ge(s_stair, n + 1)
                    pool.affine_select(out=stair[:, :, :], in_=stair[:, :, :].bitcast(F32), compare_op=ALU.not_equal,
                                       fill=1.0, base=-n * E, pattern=[[-1, E], [0, F]], channel_multiplier=1)\
                        .then_inc(s_stair, 1)

            def enter(b):
                yield WHEN["stats"][0]
                stats_ready.wait(pool, b)
                apart(pool)
                pool.tensor_scalar(var_e[:, :], mv[:, :, 1], LN_EPS, None, ALU.add).then_inc(var_ready.sem, 1)
                var_ready.wait(pool, b)
                pool.tensor_tensor(rstd[:, :], var_e[:, :], minus_half[:, :], ALU.pow).then_inc(rstd_ready.sem, 1)
                if first(b):
                    make_stairs()
                yield WHEN["keep"][0]
                if not first(b):
                    gate_ready.wait_previous(pool, b - 1)
                xh_ready.wait(pool, b)
                pool.tensor_copy(at(XH, b), xh[:, :]).then_inc(kept_x.sem, 1)
                xl_ready.wait(pool, b)
                pool.tensor_copy(at(XL, b), xl[:, :]).then_inc(kept_x.sem, 1)

            def scan(b):
                def spread_da():
                    for j in range(J):
                        yield WHEN["spread"][j]
                        da_step.wait(pool, b)
                        after(filled["between"], pool, b, j - 2) if j >= 2 else filled["between"].wait_previous(pool, b)
                        for part, spread in ((da_hi, spread_hi), (da_lo, spread_lo)):
                            pool.tensor_tensor(spread[:, j % 2, :, :], upper[:, :].unsqueeze(1).to_broadcast([P, H, P]),
                                               part[:, j, :].bitcast(F32).unsqueeze(2).to_broadcast([P, H, P]), ALU.mult)\
                                .then_inc(spread_ready.sem, 1)

                yield from spread_da()

                def chunk_inputs(j):
                    q = j % 2
                    yield SLOT["xct"][j] + 1
                    decay_ready.wait(pool, b, j)
                    smask_ready.wait(pool, b, j)
                    pool.tensor_tensor(mix[:, q, :, :], decay[:, j, :, :],
                                       smask[:, q, :].unsqueeze(1).to_broadcast([P, H, P]), ALU.mult).then_inc(mix_ready.sem, 1)
                    xdt_ready.wait(pool, b, j)
                    pool.tensor_tensor(xw[:, q, :].rearrange("p (h n) -> p h n", h=H),
                                       xdt[:, q, :].rearrange("p (h n) -> p h n", h=H),
                                       decay[:, j, :, P - 1:P].to_broadcast([P, H, HP]), ALU.mult).then_inc(xw_ready.sem, 1)

                yield from chunk_inputs(0)
                yield from chunk_inputs(1)
                for j in range(J):
                    q = j % 2
                    yield SLOT["y"][j] + 1
                    if 0 < j < J - 1:
                        grown_ready.wait(pool, b)
                        state_ready.wait(pool, b, j - 1)
                        pool.tensor_tensor(state_d[:, j - 1, :].rearrange("p (h n) -> p h n", h=H),
                                           state[:, j - 1, :].rearrange("p (h n) -> p h n", h=H),
                                           grown[0:N, 1, j, :].unsqueeze(2).to_broadcast([N, H, HP]), ALU.mult)\
                            .then_inc(stated_ready.sem, 1)
                    y_ready.wait(pool, b, j)
                    sz_ready.wait(pool, b, j)
                    pool.tensor_tensor(yg[:, q, :], y[:, q, :], sz[:, j, :], ALU.mult).then_inc(yg_ready.sem, 1)
                    if j + 2 < J:
                        yield from chunk_inputs(j + 2)
                    yield SLOT["y"][j] + 2
                    ss_ready.wait(pool, b, j)
                    apart(pool)
                    pool.tensor_scalar(sse[:, j:j + 1], ss[:, j:j + 1], 1.0 / DI, RMS_EPS, ALU.mult, ALU.add)\
                        .then_inc(rs_ready.sem, 1)
                    rs_ready.wait(pool, b, 2 * j)
                    pool.tensor_tensor(rs[:, j:j + 1], sse[:, j:j + 1], minus_half[:, 0:1], ALU.pow).then_inc(rs_ready.sem, 1)
                pool.sem_inc(stated_ready.sem, 2)

            def experts(b, mixer):
                for p in range(NQ + 1):
                    if p - 1 in POOL_LOWS:
                        take_low(pool, b, p - 1)
                    mixer.advance(p)
                mixer.advance(LAST)

            run(enter(0))
            with pool.Fori(0, NB - 1) as b:
                experts(b, Mixer(merge(scan(b), enter(b + 1))))
            experts(NB - 1, Mixer(scan(NB - 1)))

        @block.scalar
        def _(act):
            for s in (xh_ready, sz_ready, btd_ready, xraw_ready, bt_ready, ct_ready, xc_ready, tap0_done, dt_exp, dt_ln,
                      grown_ready, decay_ready, affexp_ready, cw_kept, ss_ready, ygt_ready,
                      u_read, ph_ready, gate_ready):
                s.start(act)
            act.dma_start(rows_sb[:, :], rows).then_inc(s_weights[0], 16)
            act.dma_start(conv_sb[:, :, :], conv_w).then_inc(s_weights[1], 16)
            act.dma_start(w_out_sb[:, :, :], w_out_t).then_inc(s_weights[2], 16)
            act.dma_start(land_su, ws_up).then_inc(s_weights[3], 16)
            act.dma_start(land_sd, ws_down).then_inc(s_weights[4], 16)
            act.wait_ge(s_weights[1], 16)
            act.wait_ge(s_weights[7], 16)
            act.activation(wp_hi[:, :], land_proj, ACT.Copy).then_inc(s_split_hi, 1)
            act.wait_ge(s_weights[3], 16)
            act.activation(up_hi[:, NP, 0:F], land_su, ACT.Copy).then_inc(s_split_hi, 1)
            act.wait_ge(s_weights[4], 16)
            act.activation(dn_hi[0:F, NP, :], land_sd, ACT.Copy).then_inc(s_split_hi, 1)
            act.wait_ge(s_const, CONSTANTS)
            act.activation(later[:, :], upper[:, :], ACT.Copy, scale=-1.0, bias=1.0).then_inc(s_setup, 1)
            act.wait_ge(s_weights[0], 16)
            act.activation(neg_a[:, :], rows_sb[:, E + 4:E + 8], ACT.Exp).then_inc(s_setup, 1)

            def split_high(n, src, hi):
                act.wait_ge(s_piece[n % LANDS], 16 * (n // LANDS + 1))
                act.activation(hi, land[n % LANDS], ACT.Copy).then_inc(s_split_hi, 1)

            def enter(b):
                yield SLOT["xnt"][0] + 1
                filled["xnt"].wait(act, b)
                filled["tok"].wait_previous(act, b)
                kept_x.wait_previous(act, b)
                act.activation(xh[:, :], bank_of("xnt")[:, :], ACT.Copy).then_inc(xh_ready.sem, 1)
                for j in range(J):
                    yield SLOT["tok"][j] + 1
                    filled["tok"].wait(act, b, j)
                    ps = bank_of("tok", j)
                    yg_ready.wait_previous(act, b, j)
                    act.activation(sz[:, j, :], ps[:, 0:DI], ACT.Silu).then_inc(sz_ready.sem, 1)
                    route_step.wait_previous(act, b)
                    filled["delta"].wait_previous(act, b)
                    act.activation(btd[:, j, :], ps[:, DI:TOK], ACT.Copy).then_inc(btd_ready.sem, 1)
                yield WHEN["dt_exp"][0]
                dt_step.wait(act, b, 1)
                act.activation(dtu[:, :, :], dtv[:, :, :], ACT.Exp).then_inc(dt_exp.sem, 1)
                btd_ready.wait(act, b)
                route_step.wait_previous(act, b)
                act.activation(sig[:, :, :], btd[:, :, N + H:], ACT.Exp, scale=-1.0).then_inc(affexp_ready.sem, 1)
                yield WHEN["dt_ln"][0]
                dt_exp.wait(act, b)
                act.activation(dtl[:, :, :], dtu[:, :, :], ACT.Ln, bias=1.0).then_inc(dt_ln.sem, 1)
                yield SLOT["cwt"][0] + 1
                filled["cwt"].wait(act, b)
                if not first(b):
                    gate_ready.wait_previous(act, b - 1)
                act.activation(at(CW, b), bank_of("cwt")[:, :], ACT.Copy).then_inc(cw_kept.sem, 1)

            def scan(b):
                for g in range(G):
                    yield SLOT["conv"][g] + 1
                    filled["conv"].wait(act, b, g)
                    tap_done[g].wait_previous(act, b)
                    act.activation(xraw[:, g, K - 1:], bank_of("conv", g)[:, :], ACT.Copy).then_inc(xraw_ready.sem, 1)
                    xraw_ready.wait(act, b, g)
                    filled["xct"].wait_previous(act, b)
                    act.activation(xc[:, g, :], xraw[:, g, 0:T], ACT.Identity, scale=conv_sb[:, g, 0:1]).then_inc(tap0_done.sem, 1)
                yield SLOT["bc"][0] + 1
                filled["bc"].wait(act, b)
                filled["score"].wait_previous(act, b)
                filled["y"].wait_previous(act, b)
                act.activation(bt[:, :], bank_of("bc")[0:N, :], ACT.Copy).then_inc(bt_ready.sem, 1)
                act.activation(ct[:, :], bank_of("bc")[N:2 * N, :], ACT.Copy, scale=C_SCALE).then_inc(ct_ready.sem, 1)
                def silus():
                    for g in range(G):
                        yield WHEN["xc"][g]
                        tap_done[g].wait(act, b)
                        act.activation(xc[:, g, :], xc[:, g, :], ACT.Silu).then_inc(xc_ready.sem, 1)

                def decays():
                    yield WHEN["decay"][0]
                    filled["cum"].wait(act, b)
                    yint_ready.wait_previous(act, b)
                    stated_ready.wait_previous(act, b)
                    act.activation(grown[:, :, :, :].rearrange("p a j h -> p (a j h)"), bank_of("cum")[:, 0:2 * J * H], ACT.Exp)\
                        .then_inc(grown_ready.sem, 1)
                    mix_ready.wait_previous(act, b)
                    xw_ready.wait_previous(act, b)
                    for j in range(J):
                        filled["between"].wait(act, b, j)
                        act.activation(decay[:, j, :, :].rearrange("p h t -> p (h t)"), bank_of("between", j)[:, :], ACT.Exp)\
                            .then_inc(decay_ready.sem, 1)

                yield from merge(decays(), silus())

                def transposed(j):
                    filled["ygt"].wait(act, b, j)
                    (filled["outp"].wait(act, b, j - 2) if j >= 2 else filled["outp"].wait_previous(act, b, J - 2 + j))
                    act.activation(ygt[:, j % 2, :], bank_of("ygt", j)[:, 0:DI], ACT.Copy).then_inc(ygt_ready.sem, 1)

                for j in range(J):
                    yield SLOT["y"][j] + 2
                    y_ready.wait(act, b, j)
                    if j:
                        ss_ready.wait(act, b, j - 1)
                    rs_ready.wait_previous(act, b)
                    act.activation(ysq[:, :], y[:, j % 2, :], ACT.Square, accum_out=ss[:, j:j + 1]).then_inc(ss_ready.sem, 1)
                    if j:
                        yield SLOT["ygt"][j - 1] + 1
                        transposed(j - 1)
                yield SLOT["ygt"][J - 1] + 1
                transposed(J - 1)

            def activate(b, p):
                u_filled.wait(act, b, p)
                if p < NP:
                    after(prod_ready, act, b, p - DEPTH)
                    act.activation(hid[:, p % DEPTH, :], bank[U_BANK[p % len(U_BANK)]][:, :], ACT.Silu).then_inc(u_read.sem, 1)
                else:
                    after_low(act, b, p - DEPTH)
                    act.activation(prod[0:F, p % DEPTH, :], bank[U_BANK[p % len(U_BANK)]][0:F, :], ACT.Silu).then_inc(u_read.sem, 1)

            def high(b, p):
                n = P if p < NP else F
                (prod_ready if p < NP else u_read).wait(act, b, p)
                after(down_done, act, b, p - DEPTH)
                act.activation(ph[0:n, p % DEPTH, :], prod[0:n, p % DEPTH, :], ACT.Copy).then_inc(ph_ready.sem, 1)

            def experts(b, mixer):
                for p in range(NQ):
                    activate(b, p)
                    if p:
                        high(b, p - 1)
                    mixer.advance(p)
                high(b, NP)
                mixer.advance(LAST)
                down_done.wait(act, b)
                g_filled.wait_previous(act, b)
                act.activation(gate_t[:, :], bank[Y_BANK][:, :], ACT.Silu).then_inc(gate_ready.sem, 1)

            mixer = Mixer(enter(0))
            for n, (src, hi, lo) in enumerate(SPLITS):
                split_high(n, src, hi)
                mixer.advance(SPLIT_SLOT[n])
            mixer.advance(LAST)
            act.wait_ge(s_split_lo, 3 + len(SPLITS))
            with act.Fori(0, NB - 1) as b:
                experts(b, Mixer(merge(scan(b), enter(b + 1))))
            experts(NB - 1, Mixer(scan(NB - 1)))

        @block.vector
        def _(dve):
            for s in (stats_ready, xn_ready, xl_ready, *tap_done, dt_step, biased_ready,
                      top8_ready, replaced_ready, route_step, smask_ready, xdt_ready, yint_ready, y_ready,
                      state_ready, s_kept, da_step, cw_part, prod_ready, low_ready["dve"], fin_step, fin_read):
                s.start(dve)
            def split_low(n, src, hi, lo):
                dve.wait_ge(s_split_hi, 3 + n + 1)
                dve.tensor_tensor(lo, land[n % LANDS], hi.bitcast(F32), ALU.subtract).then_inc(s_split_lo, 1)

            def enter(b):
                yield WHEN["stats"][0]
                dve.wait_ge(x_landed, b * 16 + 16)
                rstd_ready.wait_previous(dve, b)
                for j in range(J):
                    dve.bn_stats(stats[:, j, :], x_tok[:, j, :]).then_inc(stats_ready.sem, 1)
                stats_ready.wait(dve, b, J - 1)
                apart(dve)
                for j in range(J):
                    dve.bn_aggr(mv[:, j, :], stats[:, j, :]).then_inc(stats_ready.sem, 1)
                stats_ready.wait(dve, b)
                yield WHEN["xn"][0]
                rstd_ready.wait(dve, b)
                for j in range(J):
                    dve.tensor_scalar(x_tok[:, j, :], x_tok[:, j, :], mv[:, j, 0:1], rstd[:, j:j + 1],
                                      ALU.subtract, ALU.mult).then_inc(xn_ready.sem, 1)
                yield WHEN["xl"][0]
                xh_ready.wait(dve, b)
                filled["tok"].wait_previous(dve, b)
                kept_x.wait_previous(dve, b)
                dve.tensor_tensor(xl[:, :], bank_of("xnt")[:, :], xh[:, :].bitcast(F32), ALU.subtract).then_inc(xl_ready.sem, 1)

                yield WHEN["dt"][0]
                btd_ready.wait(dve, b)
                dt_exp.wait_previous(dve, b)
                dve.tensor_tensor(dtv[:, :, :], btd[:, :, N:N + H],
                                  rows_sb[:, E:E + H].unsqueeze(1).to_broadcast([P, J, H]), ALU.add).then_inc(dt_step.sem, 1)
                dt_step.wait(dve, b, 0)
                dve.tensor_scalar(dtv[:, :, :], dtv[:, :, :], DT_CAP, None, ALU.min).then_inc(dt_step.sem, 1)

                yield WHEN["dt_rest"][0]
                dt_exp.wait(dve, b)
                dve.tensor_scalar(dtw[:, :, :], dtu[:, :, :], 1.0, -1.0, ALU.add, ALU.add).then_inc(dt_step.sem, 1)
                dt_step.wait(dve, b, 2)
                dve.tensor_scalar(dtw[:, :, :], dtw[:, :, :], 1e-30, None, ALU.max).then_inc(dt_step.sem, 1)
                dt_step.wait(dve, b, 3)
                dve.reciprocal(dtr[:, :, :], dtw[:, :, :]).then_inc(dt_step.sem, 1)
                dt_ln.wait(dve, b)
                dt_step.wait(dve, b, 4)
                dve.tensor_tensor(dtr[:, :, :], dtr[:, :, :], dtu[:, :, :], ALU.mult).then_inc(dt_step.sem, 1)
                dt_step.wait(dve, b, 5)
                dve.tensor_tensor(dtr[:, :, :], dtr[:, :, :], dtl[:, :, :], ALU.mult).then_inc(dt_step.sem, 1)
                dt_step.wait(dve, b, 6)
                xdt_ready.wait_previous(dve, b)
                dve.tensor_scalar(dt_[:, :, :], dtr[:, :, :], DT_MIN, DT_MAX, ALU.max, ALU.min).then_inc(dt_step.sem, 1)
                dt_step.wait(dve, b, 7)
                filled["cum"].wait_previous(dve, b)
                spread_ready.wait_previous(dve, b)
                dve.tensor_tensor(da[:, :, :], dt_[:, :, :], neg_a[:, :].unsqueeze(1).to_broadcast([P, J, H]), ALU.mult)\
                    .then_inc(da_step.sem, 1)
                da_step.wait(dve, b, 0)
                dve.tensor_copy(da_hi[:, :, :], da[:, :, :]).then_inc(da_step.sem, 1)
                da_step.wait(dve, b, 1)
                dve.tensor_tensor(da_lo[:, :, :], da[:, :, :], da_hi[:, :, :].bitcast(F32), ALU.subtract).then_inc(da_step.sem, 1)
                dve.sem_inc(dt_step.sem, 1)

                yield WHEN["route"][0]
                btd_ready.wait(dve, b)
                replaced_ready.wait_previous(dve, b)
                dve.tensor_tensor(biased[:, :, :], btd[:, :, N + H:],
                                  rows_sb[:, 0:E].unsqueeze(1).to_broadcast([P, J, E]), ALU.add).then_inc(biased_ready.sem, 1)
                biased_ready.wait(dve, b)
                apart(dve)
                for j in range(J):
                    dve.max(top8[:, j, :], biased[:, j, :]).then_inc(top8_ready.sem, 1)
                yield WHEN["route"][1]
                for j in range(J):
                    top8_ready.wait(dve, b, j)
                    apart(dve)
                    dve.match_replace(replaced[:, j, :], top8[:, j, :], biased[:, j, :], LOWEST).then_inc(replaced_ready.sem, 1)

                def sigmoid():
                    yield WHEN["sigmoid"][0]
                    affexp_ready.wait(dve, b)
                    dve.tensor_scalar(sig[:, :, :], sig[:, :, :], 1.0, None, ALU.add).then_inc(route_step.sem, 1)
                    replaced_ready.wait(dve, b)
                    dve.tensor_tensor(replaced[:, :, :], replaced[:, :, :], biased[:, :, :], ALU.not_equal)\
                        .then_inc(route_step.sem, 1)
                    for j in range(J):
                        yield WHEN["sigmoid"][1 + j]
                        route_step.wait(dve, b, 0)
                        dve.reciprocal(sig[:, j, :], sig[:, j, :]).then_inc(route_step.sem, 1)
                    yield WHEN["sigmoid"][1 + J]
                    route_step.wait(dve, b, J + 1)
                    dve.tensor_tensor(sig[:, :, :], sig[:, :, :], replaced[:, :, :], ALU.mult).then_inc(route_step.sem, 1)
                    route_step.wait(dve, b, J + 2)
                    dve.tensor_reduce(wsum[:, :], sig[:, :, :], AX_X, ALU.add).then_inc(route_step.sem, 1)
                    yield WHEN["sigmoid"][2 + J]
                    route_step.wait(dve, b, J + 3)
                    dve.tensor_scalar(wsum[:, :], wsum[:, :], 1e-8, None, ALU.add).then_inc(route_step.sem, 1)
                    route_step.wait(dve, b, J + 4)
                    dve.reciprocal(wrec[:, :], wsum[:, :]).then_inc(route_step.sem, 1)
                    route_step.wait(dve, b, J + 5)
                    dve.tensor_tensor(sig[:, :, :], sig[:, :, :], wrec[:, :].unsqueeze(2).to_broadcast([P, J, E]), ALU.mult)\
                        .then_inc(route_step.sem, 1)
                    yield WHEN["sigmoid"][3 + J]
                    route_step.wait(dve, b, J + 6)
                    filled["cwt"].wait_previous(dve, b)
                    dve.tensor_copy(cw_cat[:, :, 0, :].bitcast(F32R), sig[:, :, :]).then_inc(cw_part.sem, 1)
                    cw_part.wait(dve, b, 0)
                    dve.tensor_tensor(cw_cat[:, :, 1, :], sig[:, :, :], cw_cat[:, :, 0, :], ALU.subtract).then_inc(cw_part.sem, 1)
                    cw_part.wait(dve, b, 1)
                    dve.sem_inc(route_step.sem, 1)

                yield from sigmoid()

            def scan(b):
                def convolve(g):
                    for k in range(1, K):
                        yield WHEN["taps"][(K - 1) * g + k - 1]
                        tap_done[g].wait(dve, b, k - 2) if k > 1 else tap0_done.wait(dve, b, g)
                        dve.scalar_tensor_tensor(xc[:, g, :], xraw[:, g, k:k + T], conv_sb[:, g, k:k + 1], xc[:, g, :],
                                                 ALU.mult, ALU.add).then_inc(tap_done[g].sem, 1)

                yield from merge(convolve(0), convolve(1))

                def chunk_inputs(j):
                    q = j % 2
                    filled["xct"].wait(dve, b, j)
                    (filled["y"].wait(dve, b, j - 2) if j >= 2 else filled["y"].wait_previous(dve, b, J - 2 + j))
                    (xw_ready.wait(dve, b, j - 2) if j >= 2 else xw_ready.wait_previous(dve, b, J - 2 + j))
                    dve.tensor_tensor(xdt[:, q, :].rearrange("p (h n) -> p h n", h=H),
                                      bank_of("xct", j)[:, 0:DI].rearrange("p (h n) -> p h n", h=H),
                                      dt_[:, j, :].unsqueeze(2).to_broadcast([P, H, HP]), ALU.mult).then_inc(xdt_ready.sem, 1)
                    filled["score"].wait(dve, b, j)
                    (mix_ready.wait(dve, b, j - 2) if j >= 2 else mix_ready.wait_previous(dve, b, J - 2 + j))
                    dve.tensor_tensor(smask[:, q, :], bank_of("score", j)[:, 0:P], upper[:, :], ALU.mult).then_inc(smask_ready.sem, 1)

                def output(j):
                    filled["outp"].wait(dve, b, j)
                    rs_ready.wait(dve, b, 2 * j + 1)
                    fin_step.wait_previous(dve, b, 0)
                    dve.tensor_scalar(S[:, j * D:(j + 1) * D], bank_of("outp", j)[:, 0:D], rs[:, j:j + 1], None, ALU.mult)\
                        .then_inc(s_kept.sem, 1)

                for j in range(2):
                    yield SLOT["xct"][j] + 1
                    chunk_inputs(j)
                for j in range(J):
                    q = j % 2
                    yield SLOT["y"][j] + 1
                    filled["y"].wait(dve, b, j)
                    ps = bank_of("y", j)
                    if j >= 2:
                        yg_ready.wait(dve, b, j - 2)
                        ss_ready.wait(dve, b, j - 2)
                    else:
                        yg_ready.wait_previous(dve, b, J - 2 + j)
                        ss_ready.wait_previous(dve, b, J - 2 + j)
                    if j:
                        grown_ready.wait(dve, b)
                        dve.tensor_tensor(yint[:, q, :].rearrange("p (h n) -> p h n", h=H),
                                          ps[:, DI:2 * DI].rearrange("p (h n) -> p h n", h=H),
                                          grown[:, 0, j, :].unsqueeze(2).to_broadcast([P, H, HP]), ALU.mult).then_inc(yint_ready.sem, 1)
                        yint_ready.wait(dve, b, j)
                        dve.tensor_tensor(y[:, q, :], ps[:, 0:DI], yint[:, q, :], ALU.add).then_inc(y_ready.sem, 1)
                    else:
                        dve.sem_inc(yint_ready.sem, 1)
                        dve.tensor_copy(y[:, q, :], ps[:, 0:DI]).then_inc(y_ready.sem, 1)
                    if j + 1 < J:
                        filled["delta"].wait(dve, b, j)
                        if j == 0:
                            filled["y"].wait_previous(dve, b)
                            stated_ready.wait_previous(dve, b)
                            dve.tensor_copy(state[:, 0, :], bank_of("delta", j)[0:N, 0:DI]).then_inc(state_ready.sem, 1)
                        else:
                            stated_ready.wait(dve, b, j - 1)
                            dve.tensor_tensor(state[:, j, :], bank_of("delta", j)[0:N, 0:DI], state_d[:, j - 1, :], ALU.add)\
                                .then_inc(state_ready.sem, 1)
                    if j:
                        yield SLOT["outp"][j - 1] + 1
                        output(j - 1)
                    if j + 2 < J:
                        yield SLOT["xct"][j + 2] + 1
                        chunk_inputs(j + 2)
                yield SLOT["outp"][J - 1] + 1
                output(J - 1)
                dve.sem_inc(state_ready.sem, 1)

            def weigh(b, p):
                u_read.wait(dve, b, p)
                c_filled.wait(dve, b, p)
                after_low(dve, b, p - DEPTH)
                dve.tensor_tensor(prod[:, p % DEPTH, :], hid[:, p % DEPTH, :], bank[C_BANK[p % len(C_BANK)]][:, :], ALU.mult)\
                    .then_inc(prod_ready.sem, 1)

            def experts(b, mixer):
                for p in range(NP):
                    weigh(b, p)
                    if p and p - 1 not in POOL_LOWS:
                        take_low(dve, b, p - 1)
                    mixer.advance(p)
                for p in (NP - 1, NP):
                    if p not in POOL_LOWS:
                        take_low(dve, b, p)
                mixer.advance(LAST)
                s_kept.wait(dve, b)
                g_filled.wait(dve, b)
                fin_read.wait_previous(dve, b)
                dve.tensor_tensor(fin[:, :, :].rearrange("p j d -> p (j d)"), S[:, :], bank[Y_BANK][:, :], ALU.mult)\
                    .then_inc(fin_step.sem, 1)
                fin_step.wait(dve, b, 0)
                dve.wait_ge(xres_landed, b * 16 + 16)
                dve.tensor_tensor(fin[:, :, :], fin[:, :, :], x_res[:, :, :], ALU.add).then_inc(fin_step.sem, 1)

            mixer = Mixer(enter(0))
            mixer.advance(max(WHEN["stats"][0], WHEN["xn"][0]))
            for n, (whole, hi, lo) in enumerate(((land_proj, wp_hi[:, :], wp_lo[:, :]),
                                                 (land_su, up_hi[:, NP, 0:F], up_lo[:, NP, 0:F]),
                                                 (land_sd, dn_hi[0:F, NP, :], dn_lo[0:F, NP, :]))):
                dve.wait_ge(s_split_hi, n + 1)
                dve.tensor_tensor(lo, whole, hi.bitcast(F32), ALU.subtract).then_inc(s_split_lo, 1)
            dve.wait_ge(s_setup, 2)
            dve.tensor_scalar(neg_a[:, :], neg_a[:, :], -1.0, None, ALU.mult).then_inc(s_setup, 1)
            dve.wait_ge(s_setup, 3)
            dve.wait_ge(s_weights[1], 16)
            for n, (src, hi, lo) in enumerate(SPLITS):
                split_low(n, src, hi, lo)
                mixer.advance(SPLIT_SLOT[n])
            mixer.advance(LAST)
            with dve.Fori(0, NB - 1) as b:
                experts(b, Mixer(merge(scan(b), enter(b + 1))))
            experts(NB - 1, Mixer(scan(NB - 1)))

        @block.tensor
        def _(pe):
            for s in (*filled.values(), u_filled, c_filled, down_done, g_filled):
                s.start(pe)

            def mm3(out_, lhs_hi, lhs_lo, rhs_hi, rhs_lo, start=True, stop=True):
                pe.matmul(out_, lhs_hi, rhs_lo, start=start, stop=False)
                pe.matmul(out_, lhs_lo, rhs_hi, start=False, stop=False)
                return pe.matmul(out_, lhs_hi, rhs_hi, start=False, stop=stop)

            pe.wait_ge(s_split_lo, 1)
            pe.wait_ge(s_setup, 3)
            pe.wait_ge(s_const, CONSTANTS)
            pe.wait_ge(s_weights[2], 16)

            def enter(b, alone=False):
                yield SLOT["xnt"][0]
                wait_bank(pe, b, "xnt", 0, alone)
                for j in range(J):
                    xn_ready.wait(pe, b, j)
                    last = pe.transpose(bank_of("xnt")[:, j * P:(j + 1) * P], x_tok[:, j, :], ident[:, :])
                last.then_inc(filled["xnt"].sem, 1)
                for j in range(J):
                    yield SLOT["tok"][j]
                    xh_ready.wait(pe, b)
                    xl_ready.wait(pe, b)
                    wait_bank(pe, b, "tok", j, alone)
                    t = slice(j * P, (j + 1) * P)
                    mm3(bank_of("tok", j)[:, 0:TOK], xh[:, t], xl[:, t], wp_hi[:, 0:TOK], wp_lo[:, 0:TOK])\
                        .then_inc(filled["tok"].sem, 1)
                yield SLOT["cwt"][0]
                wait_bank(pe, b, "cwt", 0, alone)
                cw_part.wait(pe, b)
                for j in range(J):
                    last = pe.transpose(bank_of("cwt")[:, j * P:(j + 1) * P],
                                        cw_cat[:, j, :, :].rearrange("p a e -> p (a e)"), ident[:, :])
                last.then_inc(filled["cwt"].sem, 1)

            def scan(b, alone=False):
                for g in range(G):
                    yield SLOT["conv"][g]
                    wait_bank(pe, b, "conv", g, alone)
                    c = slice(C_CONV + g * P, C_CONV + (g + 1) * P)
                    mm3(bank_of("conv", g)[:, :], wp_hi[:, c], wp_lo[:, c], at(XH, b), at(XL, b)).then_inc(filled["conv"].sem, 1)
                yield SLOT["bc"][0]
                wait_bank(pe, b, "bc", 0, alone)
                c = slice(C_BC, C_BC + 2 * N)
                mm3(bank_of("bc")[:, :], wp_hi[:, c], wp_lo[:, c], at(XH, b), at(XL, b)).then_inc(filled["bc"].sem, 1)

                yield SLOT["cum"][0]
                wait_bank(pe, b, "cum", 0, alone)
                da_step.wait(pe, b)
                da_flat = da[:, :, :].rearrange("p j h -> p (j h)")
                pe.matmul(bank_of("cum")[:, 0:J * H], upper[:, :], da_flat, start=True, stop=True)
                pe.matmul(bank_of("cum")[:, J * H:2 * J * H], ones[:, :], da_flat, start=True, stop=True)\
                    .then_inc(filled["cum"].sem, 1)
                for j in range(J):
                    yield SLOT["between"][j]
                    wait_bank(pe, b, "between", j, alone)
                    spread_ready.wait(pe, b, 2 * j + 1)
                    o = bank_of("between", j)[:, :]
                    pe.matmul(o, later[:, :], spread_lo[:, j % 2, :, :].rearrange("p h t -> p (h t)"), start=True, stop=False)
                    pe.matmul(o, later[:, :], spread_hi[:, j % 2, :, :].rearrange("p h t -> p (h t)"), start=False, stop=True)\
                        .then_inc(filled["between"].sem, 1)

                def chunk_inputs(j):
                    t = slice(j * P, (j + 1) * P)
                    wait_bank(pe, b, "xct", j, alone)
                    for g in range(G):
                        xc_ready.wait(pe, b, g)
                        last = pe.transpose(bank_of("xct", j)[:, g * P:(g + 1) * P], xc[:, g, t], ident[:, :])
                    last.then_inc(filled["xct"].sem, 1)
                    wait_bank(pe, b, "score", j, alone)
                    bt_ready.wait(pe, b)
                    ct_ready.wait(pe, b)
                    pe.matmul(bank_of("score", j)[:, 0:P], bt[:, t], ct[:, t], start=True, stop=True)\
                        .then_inc(filled["score"].sem, 1)

                def gated_transpose(j):
                    q = j % 2
                    wait_bank(pe, b, "ygt", j, alone)
                    yg_ready.wait(pe, b, j)
                    for g in range(G):
                        last = pe.transpose(bank_of("ygt", j)[:, g * P:(g + 1) * P], yg[:, q, g * P:(g + 1) * P], ident[:, :])
                    last.then_inc(filled["ygt"].sem, 1)

                def project(j):
                    q = j % 2
                    wait_bank(pe, b, "outp", j, alone)
                    ygt_ready.wait(pe, b, j)
                    for g in range(G):
                        last = pe.matmul(bank_of("outp", j)[:, 0:D], ygt[:, q, g * P:(g + 1) * P], w_out_sb[:, g, :],
                                         start=(g == 0), stop=(g == G - 1))
                    last.then_inc(filled["outp"].sem, 1)

                for j in range(2):
                    yield SLOT["xct"][j]
                    chunk_inputs(j)
                for j in range(J):
                    q = j % 2
                    t = slice(j * P, (j + 1) * P)
                    yield SLOT["y"][j]
                    wait_bank(pe, b, "y", j, alone)
                    xdt_ready.wait(pe, b, j)
                    mix_ready.wait(pe, b, j)
                    ps = bank_of("y", j)
                    for h in range(H):
                        last = pe.matmul(ps[:, h * HP:(h + 1) * HP], mix[:, q, h, :], xdt[:, q, h * HP:(h + 1) * HP],
                                         start=True, stop=True)
                    if j:
                        state_ready.wait(pe, b, j - 1)
                        last = pe.matmul(ps[:, DI:2 * DI], ct[:, t], state[:, j - 1, :], start=True, stop=True)
                    last.then_inc(filled["y"].sem, 1)
                    if j + 1 < J:
                        wait_bank(pe, b, "delta", j, alone)
                        xw_ready.wait(pe, b, j)
                        pe.matmul(bank_of("delta", j)[0:N, 0:DI], btd[:, j, 0:N], xw[:, q, :], start=True, stop=True)\
                            .then_inc(filled["delta"].sem, 1)
                    if j:
                        yield SLOT["ygt"][j - 1]
                        gated_transpose(j - 1)
                        yield SLOT["outp"][j - 1]
                        project(j - 1)
                    if j + 2 < J:
                        yield SLOT["xct"][j + 2]
                        chunk_inputs(j + 2)
                yield SLOT["ygt"][J - 1]
                gated_transpose(J - 1)
                yield SLOT["outp"][J - 1]
                project(J - 1)

            def up(b, p):
                after(u_read, pe, b, p - len(U_BANK))
                n = P if p < NP else F
                if p == NP:
                    apart(pe)
                mm3(bank[U_BANK[p % len(U_BANK)]][0:n, :], up_hi[:, p, 0:n], up_lo[:, p, 0:n], at(XH, b), at(XL, b))\
                    .then_inc(u_filled.sem, 1)

            def weights(b, p):
                after(prod_ready, pe, b, p - len(C_BANK))
                pe.matmul(bank[C_BANK[p % len(C_BANK)]][:, :], stair[:, 2 * p:2 * p + 2, :].rearrange("p e f -> p (e f)"),
                          at(CW, b), start=True, stop=True).then_inc(c_filled.sem, 1)

            def down(b, p):
                ph_ready.wait(pe, b, p)
                after_low(pe, b, p)
                if p == 0:
                    fin_step.wait_previous(pe, b, 0)
                n = P if p < NP else F
                mm3(bank[Y_BANK][:, :], dn_hi[0:n, p, :], dn_lo[0:n, p, :], ph[0:n, p % DEPTH, :], pl[0:n, p % DEPTH, :],
                    start=(p == 0), stop=(p == NP)).then_inc(down_done.sem, 1)

            def experts(b, mixer):
                for p in range(NQ + DEPTH):
                    if p + len(U_BANK) < NQ:
                        up(b, p + len(U_BANK))
                    if p + len(C_BANK) < NP:
                        weights(b, p + len(C_BANK))
                    for q in range(NQ):
                        if DOWN_SLOT[q] == p:
                            down(b, q)
                    mixer.advance(p)
                mixer.advance(LAST)

            def begin(b):
                kept_x.wait(pe, b)
                for p in range(len(U_BANK)):
                    up(b, p)
                cw_kept.wait(pe, b)
                for p in range(len(C_BANK)):
                    weights(b, p)

            def gate(b):
                gate_ready.wait(pe, b)
                for j in range(J):
                    last = pe.transpose(bank[Y_BANK][:, j * P:(j + 1) * P], gate_t[:, j * P:(j + 1) * P], ident[:, :])
                last.then_inc(g_filled.sem, 1)

            run(enter(0, alone=True))
            pe.wait_ge(s_split_lo, 3 + len(SPLITS))
            pe.wait_ge(s_stair, 3)
            begin(0)
            with pe.Fori(0, NB - 1) as b:
                experts(b, Mixer(merge(scan(b), enter(b + 1))))
                begin(b + 1)
                gate(b)
            experts(NB - 1, Mixer(scan(NB - 1, alone=True)))
            gate(NB - 1)


def kernel(**inputs):
    import numpy as np
    import concourse.bacc as bacc
    from concourse.bass_utils import run_bass_kernel_spmd

    a = {k: np.asarray(v) for k, v in inputs.items()}
    w_in = a["L0_attn_W_in"].T
    w_out = a["L0_attn_W_out"].T
    cent = a["L0_ffn_centroids"].T
    D, DI = w_in.shape[0], w_out.shape[0]
    E, _, F = a["L0_ffn_W_up"].shape
    H = a["L0_attn_A_log"].shape[0]
    N = (w_in.shape[1] - 2 * DI - H) // 2
    z, xc, B, C, dt = np.split(w_in, [DI, 2 * DI, 2 * DI + N, 2 * DI + 2 * N], axis=1)
    row = np.concatenate([a["L0_ffn_expert_biases"], a["L0_attn_dt_bias"], a["L0_attn_A_log"]])
    arrays = {
        "x": a["L0_attn_x"],
        "w_proj": np.concatenate([z, B, dt, cent, xc, B, C], axis=1),
        "w_out_t": w_out.reshape(DI // 128, 128, D).transpose(1, 0, 2),
        "conv_w": a["L0_attn_conv_w"].reshape(DI // 128, 128, -1).transpose(1, 0, 2),
        "rows": np.broadcast_to(row, (128, row.size)),
        "w_up": a["L0_ffn_W_up"].transpose(1, 0, 2).reshape(D, E * F),
        "w_down": a["L0_ffn_W_down"].reshape(E // 2, 2 * F, D).transpose(1, 0, 2).reshape(2 * F, (E // 2) * D),
        "ws_up": a["L0_ffn_Ws_up"],
        "ws_down": a["L0_ffn_Ws_down"],
    }
    arrays = {k: np.ascontiguousarray(v) for k, v in arrays.items()}
    nc = bacc.Bacc("TRN2", target_bir_lowering=False, num_devices=1)
    args = [nc.dram_tensor(k, v.shape, F32, kind="ExternalInput").ap() for k, v in arrays.items()]
    out = nc.dram_tensor("out", a["L0_attn_x"].shape, F32, kind="ExternalOutput").ap()
    build(nc, *args, out)
    r = run_bass_kernel_spmd(nc, [arrays], core_ids=[0])
    return r.results[0]["out"]
```

```python
from contextlib import ExitStack

import concourse.bass as bass
from concourse import mybir

F32 = mybir.dt.float32
F32R = mybir.dt.float32r
ALU = mybir.AluOpType
ACT = mybir.ActivationFunctionType
AX_X = mybir.AxisListType.X

P = 128
LOWEST = -3.4028234e38
LN_EPS = 1e-5
RMS_EPS = 1.1920929e-07
DT_MIN, DT_MAX = 1e-4, 0.5
DT_CAP = 1.0
LN_ODD = (11, 9, 7, 5, 3, 1)
RING = 3
DEPTH = 4
HIDS = 3


class Signal:

    def __init__(self, sem, per):
        self.sem, self.per = sem, per

    def start(self, eng):
        eng.sem_inc(self.sem, self.per)

    def wait(self, eng, b, k=None):
        k = self.per - 1 if k is None else k
        eng.wait_ge(self.sem, b * self.per + (self.per + k + 1))

    def wait_previous(self, eng, b, k=None):
        k = self.per - 1 if k is None else k
        eng.wait_ge(self.sem, b * self.per + (k + 1))




def build(nc, x, w_proj, w_out_t, conv_w, rows, w_up, w_down, ws_up, ws_down, out):
    NB, T, D = x.shape
    J = T // P
    E = rows.shape[1] - 8
    H = 4
    DI = 2 * D
    HP = DI // H
    N = (w_proj.shape[1] - 2 * DI - H - E) // 3
    F = ws_up.shape[1]
    NP = E // 2
    G = DI // P
    K = 4
    C_SCALE = float(N) ** -0.5
    TOK = DI + N + H + E
    BTD = N + H + E
    assert D == P and HP * H == DI and 2 * F == P and N == 64

    ctx = ExitStack()
    with ctx:
        def sb(name, shape, dt=F32):
            return ctx.enter_context(nc.sbuf_tensor(name, shape, dt))

        def sem(name):
            return ctx.enter_context(nc.semaphore(name))

        def signal(name, per):
            return Signal(sem(name), per)

        up_hi, up_lo = sb("up_hi", [P, NP + 1, P], F32R), sb("up_lo", [P, NP + 1, P], F32R)
        dn_hi, dn_lo = sb("dn_hi", [P, NP + 1, D], F32R), sb("dn_lo", [P, NP + 1, D], F32R)
        wp_hi, wp_lo = sb("wp_hi", [P, w_proj.shape[1]], F32R), sb("wp_lo", [P, w_proj.shape[1]], F32R)
        w_out_sb = sb("w_out_sb", [P, G, D])
        conv_sb = sb("conv_sb", [P, G, K])
        rows_sb = sb("rows_sb", [P, E + 8])
        neg_a = sb("neg_a", [P, H])
        ident = sb("ident", [P, P])
        upper = sb("upper", [P, P])
        ones = sb("ones", [P, P])
        later = sb("later", [P, P], F32R)
        stair = sb("stair", [P, E, F], F32R)
        minus_half = sb("minus_half", [P, J])
        XH, XL = sb("XH", [P, 2, T], F32R), sb("XL", [P, 2, T], F32R)
        CW = sb("CW", [P, 2, T], F32R)
        S = sb("S", [P, J * D])
        x_tok = sb("x_tok", [P, J, D])
        stats = sb("stats", [P, J, 6])
        mv = sb("mv", [P, J, 2])
        var_e = sb("var_e", [P, J])
        rstd = sb("rstd", [P, J])
        xh, xl = sb("xh", [P, T], F32R), sb("xl", [P, T], F32R)
        sz = sb("sz", [P, J, DI])
        btd = sb("btd", [P, J, BTD])
        xraw = sb("xraw", [P, G, T + K - 1])
        xc = sb("xc", [P, G, T])
        bt, ct = sb("bt", [N, T]), sb("ct", [N, T])
        dtv = sb("dtv", [P, J, H])
        dtu, dtl = sb("dtu", [P, J, H]), sb("dtl", [P, J, H])
        dts, dtq = sb("dts", [P, J, H]), sb("dtq", [P, J, H])
        dtr, dt_ = sb("dtr", [P, J, H]), sb("dt_", [P, J, H])
        da = sb("da", [P, J, H])
        da_hi, da_lo = sb("da_hi", [P, J, H], F32R), sb("da_lo", [P, J, H], F32R)
        spread_hi, spread_lo = sb("spread_hi", [P, 2, H, P], F32R), sb("spread_lo", [P, 2, H, P], F32R)
        grown = sb("grown", [P, 2, J, H])
        decay = sb("decay", [P, J, H, P])
        biased, top8, replaced = sb("biased", [P, J, E]), sb("top8", [P, J, 8]), sb("replaced", [P, J, E])
        sig = sb("sig", [P, J, E])
        wsum, wrec = sb("wsum", [P, J]), sb("wrec", [P, J])
        cw_cat = sb("cw_cat", [P, J, 2, E])
        smask = sb("smask", [P, 2, P])
        mix = sb("mix", [P, 2, H, P])
        xdt, xw = sb("xdt", [P, 2, DI]), sb("xw", [P, 2, DI])
        yint, y = sb("yint", [P, 2, DI]), sb("y", [P, 2, DI])
        ss, rs = sb("ss", [P, J]), sb("rs", [P, J])
        sse = sb("sse", [P, J])
        yg = sb("yg", [P, 2, DI])
        ygt = sb("ygt", [P, 2, DI])
        state, state_d = sb("state", [N, J - 1, DI]), sb("state_d", [N, J - 2, DI])
        hid, prod = sb("hid", [P, HIDS, T]), sb("prod", [P, DEPTH, T])
        ph, pl = sb("ph", [P, DEPTH, T], F32R), sb("pl", [P, DEPTH, T], F32R)
        gate_t = sb("gate_t", [P, T])
        x_res = sb("x_res", [P, J, D])

        bank = [ctx.enter_context(nc.psum_tensor(f"bank{i}", [P, 512], F32)) for i in range(8)]
        U_BANK, C_BANK, Y_BANK = (3, 4), (5, 6), 7
        C_LEAD = 2

        SCAN = [("conv", g) for g in range(G)] + [("bc", 0), ("cum", 0)] + [("between", j) for j in range(J)]
        SCAN += [("xct", 0), ("score", 0), ("xct", 1), ("score", 1)]
        for j in range(J):
            SCAN += [("y", j)]
            if j + 1 < J:
                SCAN += [("delta", j)]
            if j:
                SCAN += [("ygt", j - 1), ("outp", j - 1)]
            if j + 2 < J:
                SCAN += [("xct", j + 2), ("score", j + 2)]
        SCAN += [("ygt", J - 1), ("outp", J - 1)]
        ENTER = [("xnt", 0)] + [("tok", j) for j in range(J)] + [("cwt", 0)]
        SLOT = {"conv": [1, 1], "bc": [2], "cum": [2], "between": [2, 3, 4, 4], "xct": [7, 10, 14, 19],
                "score": [7, 10, 14, 19], "y": [12, 15, 19, 22], "delta": [12, 15, 19], "ygt": [17, 19, 22, 25],
                "outp": [19, 22, 24, 30], "xnt": [15], "tok": [20, 21, 21, 23], "cwt": [33]}
        DOWN_SLOT = [2, 3, 4, 4, 5, 6, 8, 9, 11, 12, 12, 13, 15, 16, 16, 18, 19, 20, 20, 20, 24, 24, 24, 25, 26,
                     27, 30, 31, 31, 32, 33, 35, 35]
        WHEN = {"taps": [2, 3, 4, 4, 3, 5], "xc": [5, 7], "spread": [0, 1, 3, 4], "decay": [6], "stats": [12],
                "xn": [15], "xl": [16], "keep": [21], "dt": [24], "dt_exp": [25], "dt_rest": [32], "route": [24, 25],
                "sigmoid": [24, 26, 27, 28, 29, 29, 30, 30]}

        def slot_of(fill):
            return SLOT[fill[0]][fill[1]]

        assert SCAN == sorted(SCAN, key=slot_of) and ENTER == sorted(ENTER, key=slot_of)
        FILLS = sorted(SCAN + ENTER, key=slot_of)
        place = {f: n for n, f in enumerate(FILLS)}
        per = {}
        for name, _ in FILLS:
            per[name] = per.get(name, 0) + 1
        filled = {name: signal(f"{name}_in_psum", n) for name, n in per.items()}

        def bank_of(name, k=0):
            return bank[place[name, k] % RING]

        def wait_bank(pe, b, name, k=0, alone=False):
            part = ENTER if (name, k) in ENTER else SCAN
            n = place[name, k] - RING
            while alone and n >= 0 and FILLS[n] not in part:
                n -= RING
            if alone and n < 0 and part is ENTER:
                return
            turn = 0
            if n < 0:
                turn = -1
                n = max(m for m in range(len(FILLS)) if (m - place[name, k]) % RING == 0)
            before, i = FILLS[n]
            apart_by = turn + (FILLS[n] in ENTER) - ((name, k) in ENTER)
            assert apart_by >= -1
            if apart_by < 0:
                readers[before].wait_previous(pe, b, i)
            else:
                readers[before].wait(pe, b + apart_by if apart_by else b, i)

        rows_landed, conv_landed, w_out_landed = sem("rows_landed"), sem("conv_w_landed"), sem("w_out_landed")
        ws_up_landed, ws_down_landed, w_proj_landed = sem("ws_up_landed"), sem("ws_down_landed"), sem("w_proj_landed")
        s_piece = [sem(f"expert_weights_{i}_landed") for i in range(5)]
        s_const = sem("constants_made")
        s_split_hi, s_split_lo = sem("weight_high_parts_made"), sem("weight_low_parts_made")
        s_split_lo_pool = sem("weight_low_parts_made_by_pool")
        s_setup = sem("setup_made")
        s_stair = sem("stairs_made")
        s_passed = sem("lone_waits_passed")
        x_landed = sem("x_landed")
        stats_ready = signal("stats_ready", 2 * J)
        var_ready, rstd_ready = signal("var_ready", 1), signal("rstd_ready", 1)
        xn_ready = signal("xn_ready", J)
        xh_ready, xl_ready = signal("xh_ready", 1), signal("xl_ready", 1)
        kept_x = signal("xh_xl_kept", 2)
        sz_ready, btd_ready = signal("silu_z_ready", J), signal("btd_ready", J)
        xraw_ready = signal("xraw_ready", G)
        bt_ready, ct_ready = signal("bt_ready", 1), signal("ct_ready", 1)
        tap_done = [signal(f"conv_{g}_tap_done", K - 1) for g in range(G)]
        tap0_done = signal("first_taps_done", G)
        xc_ready = signal("xc_ready", G)
        dt_step, dt_exp = signal("dt_step_done", 8 + len(LN_ODD)), signal("dt_exp_ready", 1)
        spread_ready = signal("spread_ready", 2 * J)
        grown_ready, decay_ready = signal("decay_from_start_ready", 1), signal("decay_ready", J)
        da_step, cw_part = signal("da_step_done", 3), signal("cw_part_done", 2)
        biased_ready, top8_ready = signal("biased_ready", 1), signal("top8_ready", J)
        replaced_ready = signal("replaced_ready", J)
        affexp_ready, route_step = signal("affinity_exp_ready", 1), signal("route_step_done", J + 8)
        cw_kept = signal("cw_kept", 1)
        smask_ready, mix_ready = signal("masked_scores_ready", J), signal("mix_ready", J)
        xdt_ready, xw_ready = signal("xdt_ready", J), signal("xw_ready", J)
        yint_ready, y_ready = signal("y_inter_ready", J), signal("y_ready", J)
        ss_ready, rs_ready = signal("y_square_sum_ready", J), signal("y_rstd_ready", 2 * J)
        yg_ready, ygt_ready = signal("gated_y_ready", J), signal("gated_y_t_ready", J)
        stated_ready, state_ready = signal("state_decayed", J), signal("state_ready", J)
        s_kept = signal("s_kept", J)
        readers = {"xnt": xl_ready, "tok": btd_ready, "conv": xraw_ready, "bc": ct_ready, "cum": grown_ready,
                   "between": decay_ready, "cwt": cw_kept, "xct": xdt_ready, "score": smask_ready, "y": y_ready,
                   "delta": state_ready, "ygt": ygt_ready, "outp": s_kept}
        NQ = NP + 1
        u_filled, u_read = signal("up_in_psum", NQ), signal("hidden_ready", NQ)
        c_filled = signal("weights_in_psum", NP)
        prod_ready = signal("weighted_hidden_ready", NP)
        DVE_HIGHS = [5, 14, 18, 21, 24]
        high_of = [("dve", DVE_HIGHS.index(p)) if p in DVE_HIGHS else ("act", p - sum(q < p for q in DVE_HIGHS))
                   for p in range(NQ)]
        high_ready = {"dve": signal("high_part_from_dve_ready", len(DVE_HIGHS)),
                      "act": signal("high_part_from_act_ready", NQ - len(DVE_HIGHS))}
        POOL_LOWS = [3, 4, 7, 9, 11, 19, 20, 23, 24, 25, 26, 27, 28, 29]
        low_of = [("pool", POOL_LOWS.index(p)) if p in POOL_LOWS else ("dve", p - sum(q < p for q in POOL_LOWS))
                  for p in range(NQ)]
        low_ready = {"pool": signal("low_part_from_pool_ready", len(POOL_LOWS)),
                     "dve": signal("low_part_from_dve_ready", NQ - len(POOL_LOWS))}
        down_done = signal("down_product_done", NQ)
        gate_ready = signal("gate_t_ready", 1)
        g_filled = signal("gate_in_psum", 1)
        fin_step, fin_read = signal("result_step_done", 2), signal("result_stored", 1)
        xres_landed = sem("x_residual_landed")
        stored = sem("result_landed_in_dram")

        block = ctx.enter_context(nc.Block())

        def at(tile, b):
            return tile[:, bass.ds(b % 2, 1), :].rearrange("p a t -> p (a t)")

        def apart(eng):
            eng.sem_inc(s_passed, 1)

        CONSTANTS = 7
        SPLIT_SLOT = [17, 18, 21, 25, 28, 27, 29, 32]

        def merge(*parts):
            parts = [[next(part), part] for part in parts]
            while parts:
                head = min(parts, key=lambda part: part[0])
                yield head[0]
                head[0] = next(head[1], None)
                if head[0] is None:
                    parts.remove(head)

        class Mixer:

            def __init__(self, steps):
                self.steps, self.slot = steps, next(steps)

            def advance(self, p):
                while self.slot <= p:
                    self.slot = next(self.steps, LAST + 1)

        def run(steps):
            for _ in steps:
                pass

        LAST = 10 ** 5

        def after(signal_, eng, b, k):
            if k >= 0:
                signal_.wait(eng, b, k)
            else:
                signal_.wait_previous(eng, b)

        def wait_low(eng, b, p):
            who, k = low_of[p]
            low_ready[who].wait(eng, b, k)

        def after_low(eng, b, p):
            if p >= DEPTH:
                wait_low(eng, b, p - DEPTH)
            else:
                who, k = low_of[max(q for q in range(NQ) if (q - p) % DEPTH == 0)]
                low_ready[who].wait_previous(eng, b, k)

        def wait_high(eng, b, p):
            who, k = high_of[p]
            high_ready[who].wait(eng, b, k)

        def take_low(eng, b, p):
            n = P if p < NP else F
            wait_high(eng, b, p)
            after(down_done, eng, b, p - DEPTH)
            eng.tensor_tensor(pl[0:n, p % DEPTH, :], prod[0:n, p % DEPTH, :], ph[0:n, p % DEPTH, :].bitcast(F32),
                              ALU.subtract).then_inc(low_ready[low_of[p][0]].sem, 1)

        def first(b):
            return isinstance(b, int) and b == 0

        x_view = x.rearrange("b (j p) d -> b p j d", p=P)
        out_view = out.rearrange("b (j p) d -> b p j d", p=P)

        def dram_at(view, b):
            return view[bass.ds(b, 1), :, :, :].rearrange("a p j d -> (a p) j d")

        C_CONV, C_BC = TOK, TOK + DI
        WP = w_proj.shape[1]
        QUARTER = NP // 4

        land = [decay[:, 0:2, :, :].rearrange("p j h t -> p (j h t)"),
                decay[:, 2:4, :, :].rearrange("p j h t -> p (j h t)"),
                xc[:, :, :].rearrange("p g t -> p (g t)"),
                hid[:, 0:2, :].rearrange("p a t -> p (a t)"), prod[:, 0:2, :].rearrange("p a t -> p (a t)")]
        LANDS = len(land)
        land_proj = mix[:, :, :, :].rearrange("p a h t -> p (a h t)")[:, 0:WP]
        land_su, land_sd = gate_t[:, 0:F], gate_t[0:F, P:P + D]
        SPLITS = []
        for dram, hi, lo in ((w_up, up_hi, up_lo), (w_down, dn_hi, dn_lo)):
            for q in range(0, NP, QUARTER):
                SPLITS.append((dram[:, q * P:(q + QUARTER) * P], hi[:, q:q + QUARTER, :].rearrange("p a t -> p (a t)"),
                               lo[:, q:q + QUARTER, :].rearrange("p a t -> p (a t)")))

        POOL_SPLITS = [4, 5, 6, 7]

        def split_low(eng, n):
            src, hi, lo = SPLITS[n]
            eng.wait_ge(s_split_hi, 3 + n + 1)
            eng.tensor_tensor(lo, land[n % LANDS], hi.bitcast(F32), ALU.subtract)\
                .then_inc(s_split_lo_pool if n in POOL_SPLITS else s_split_lo, 1)

        def wait_up_splits(eng):
            eng.wait_ge(s_split_lo, 3 + len(SPLITS) // 2)
            eng.wait_ge(s_split_lo_pool, 1)

        def wait_splits(eng):
            eng.wait_ge(s_split_lo, 3 + len(SPLITS) - len(POOL_SPLITS))
            eng.wait_ge(s_split_lo_pool, len(POOL_SPLITS))

        @block.sync
        def _(sp):
            def load(b):
                filled["xnt"].wait_previous(sp, b)
                sp.dma_start(x_tok[:, :, :], dram_at(x_view, b)).then_inc(x_landed, 16)

            def finish(b):
                fin_step.wait_previous(sp, b)
                sp.dma_start(x_res[:, :, :], dram_at(x_view, b)).then_inc(xres_landed, 16)
                fin_step.wait(sp, b)
                sp.dma_start(dram_at(out_view, b), S[:, :].rearrange("p (j d) -> p j d", j=J)).then_inc(stored, 16)
                sp.wait_ge(stored, b * 16 + 16)
                sp.sem_inc(fin_read.sem, 1)

            load(0)
            sp.dma_start(land_proj, w_proj).then_inc(w_proj_landed, 16)
            for n, (src, hi, lo) in enumerate(SPLITS):
                if n >= LANDS:
                    sp.wait_ge(s_split_lo, n - LANDS + 1 + 3)
                sp.dma_start(land[n % LANDS], src).then_inc(s_piece[n % LANDS], 16)
            load(1)
            with sp.Fori(0, NB - 2) as b:
                load(b + 2)
                finish(b)
            finish(NB - 2)
            finish(NB - 1)

        @block.gpsimd
        def _(pool):
            for s in (var_ready, rstd_ready, kept_x, xw_ready, mix_ready, yg_ready, rs_ready, stated_ready,
                      spread_ready, low_ready["pool"]):
                s.start(pool)
            pool.memset(ident[:, :], 0.0).then_inc(s_const, 1)
            pool.memset(upper[:, :], 1.0).then_inc(s_const, 1)
            pool.memset(ones[:, :], 1.0).then_inc(s_const, 1)
            pool.memset(minus_half[:, :], -0.5).then_inc(s_const, 1)
            pool.memset(xraw[:, :, 0:K - 1], 0.0).then_inc(s_const, 1)
            pool.wait_ge(s_const, 5)
            pool.affine_select(out=ident[:, :], in_=ident[:, :], compare_op=ALU.not_equal, fill=1.0, base=0,
                               pattern=[[-1, P]], channel_multiplier=1).then_inc(s_const, 1)
            pool.affine_select(out=upper[:, :], in_=upper[:, :], compare_op=ALU.is_ge, fill=0.0, base=0,
                               pattern=[[1, P]], channel_multiplier=-1).then_inc(s_const, 1)

            pool.memset(stair[:, :, :].rearrange("p e f -> p (e f)").bitcast(F32), 0.0).then_inc(s_stair, 1)

            def make_stair(n):
                pool.wait_ge(s_stair, n + 1)
                pool.affine_select(out=stair[:, :, :], in_=stair[:, :, :].bitcast(F32), compare_op=ALU.not_equal,
                                   fill=1.0, base=-n * E, pattern=[[-1, E], [0, F]], channel_multiplier=1)\
                    .then_inc(s_stair, 1)

            def enter(b):
                yield WHEN["stats"][0]
                stats_ready.wait(pool, b)
                apart(pool)
                pool.tensor_scalar(var_e[:, :], mv[:, :, 1], LN_EPS, None, ALU.add).then_inc(var_ready.sem, 1)
                var_ready.wait(pool, b)
                pool.tensor_tensor(rstd[:, :], var_e[:, :], minus_half[:, :], ALU.pow).then_inc(rstd_ready.sem, 1)
                yield WHEN["keep"][0]
                if not first(b):
                    gate_ready.wait_previous(pool, b - 1)
                xh_ready.wait(pool, b)
                pool.tensor_copy(at(XH, b), xh[:, :]).then_inc(kept_x.sem, 1)
                xl_ready.wait(pool, b)
                pool.tensor_copy(at(XL, b), xl[:, :]).then_inc(kept_x.sem, 1)

            def scan(b):
                def spread_da():
                    for j in range(J):
                        yield WHEN["spread"][j]
                        da_step.wait(pool, b)
                        after(filled["between"], pool, b, j - 2) if j >= 2 else filled["between"].wait_previous(pool, b)
                        for part, spread in ((da_hi, spread_hi), (da_lo, spread_lo)):
                            pool.tensor_tensor(spread[:, j % 2, :, :], upper[:, :].unsqueeze(1).to_broadcast([P, H, P]),
                                               part[:, j, :].bitcast(F32).unsqueeze(2).to_broadcast([P, H, P]), ALU.mult)\
                                .then_inc(spread_ready.sem, 1)

                yield from spread_da()

                def chunk_inputs(j):
                    q = j % 2
                    yield SLOT["xct"][j] + 1
                    decay_ready.wait(pool, b, j)
                    smask_ready.wait(pool, b, j)
                    pool.tensor_tensor(mix[:, q, :, :], decay[:, j, :, :],
                                       smask[:, q, :].unsqueeze(1).to_broadcast([P, H, P]), ALU.mult).then_inc(mix_ready.sem, 1)
                    xdt_ready.wait(pool, b, j)
                    pool.tensor_tensor(xw[:, q, :].rearrange("p (h n) -> p h n", h=H),
                                       xdt[:, q, :].rearrange("p (h n) -> p h n", h=H),
                                       decay[:, j, :, P - 1:P].to_broadcast([P, H, HP]), ALU.mult).then_inc(xw_ready.sem, 1)

                yield from chunk_inputs(0)
                yield from chunk_inputs(1)
                for j in range(J):
                    q = j % 2
                    yield SLOT["y"][j] + 1
                    if 0 < j < J - 1:
                        grown_ready.wait(pool, b)
                        state_ready.wait(pool, b, j - 1)
                        pool.tensor_tensor(state_d[:, j - 1, :].rearrange("p (h n) -> p h n", h=H),
                                           state[:, j - 1, :].rearrange("p (h n) -> p h n", h=H),
                                           grown[0:N, 1, j, :].unsqueeze(2).to_broadcast([N, H, HP]), ALU.mult)\
                            .then_inc(stated_ready.sem, 1)
                    y_ready.wait(pool, b, j)
                    sz_ready.wait(pool, b, j)
                    pool.tensor_tensor(yg[:, q, :], y[:, q, :], sz[:, j, :], ALU.mult).then_inc(yg_ready.sem, 1)
                    if j + 2 < J:
                        yield from chunk_inputs(j + 2)
                    yield SLOT["y"][j] + 2
                    ss_ready.wait(pool, b, j)
                    apart(pool)
                    pool.tensor_scalar(sse[:, j:j + 1], ss[:, j:j + 1], 1.0 / DI, RMS_EPS, ALU.mult, ALU.add)\
                        .then_inc(rs_ready.sem, 1)
                    rs_ready.wait(pool, b, 2 * j)
                    pool.tensor_tensor(rs[:, j:j + 1], sse[:, j:j + 1], minus_half[:, 0:1], ALU.pow).then_inc(rs_ready.sem, 1)
                pool.sem_inc(stated_ready.sem, 2)

            def experts(b, mixer):
                for p in range(NQ + 1):
                    if p - 1 in POOL_LOWS:
                        take_low(pool, b, p - 1)
                    mixer.advance(p)
                mixer.advance(LAST)
                fin_step.wait(pool, b, 0)
                pool.wait_ge(xres_landed, b * 16 + 16)
                pool.tensor_tensor(S[:, :], S[:, :], x_res[:, :, :].rearrange("p j d -> p (j d)"), ALU.add)\
                    .then_inc(fin_step.sem, 1)

            mixer = Mixer(enter(0))
            mixer.advance(max(WHEN["stats"][0], WHEN["xn"][0]))
            make_stair(0)
            make_stair(1)
            mixer.advance(LAST)
            for n in POOL_SPLITS:
                split_low(pool, n)
            with pool.Fori(0, NB - 1) as b:
                experts(b, Mixer(merge(scan(b), enter(b + 1))))
            experts(NB - 1, Mixer(scan(NB - 1)))

        @block.scalar
        def _(act):
            for s in (xh_ready, sz_ready, btd_ready, xraw_ready, bt_ready, ct_ready, xc_ready, tap0_done, dt_exp,
                      grown_ready, decay_ready, affexp_ready, cw_kept, ss_ready, ygt_ready,
                      u_read, high_ready["act"], gate_ready):
                s.start(act)
            act.dma_start(rows_sb[:, :], rows).then_inc(rows_landed, 16)
            act.dma_start(conv_sb[:, :, :], conv_w).then_inc(conv_landed, 16)
            act.dma_start(w_out_sb[:, :, :], w_out_t).then_inc(w_out_landed, 16)
            act.dma_start(land_su, ws_up).then_inc(ws_up_landed, 16)
            act.dma_start(land_sd, ws_down).then_inc(ws_down_landed, 16)
            act.wait_ge(w_proj_landed, 16)
            act.activation(wp_hi[:, :], land_proj, ACT.Copy).then_inc(s_split_hi, 1)

            def split_high(n, src, hi):
                act.wait_ge(s_piece[n % LANDS], 16 * (n // LANDS + 1))
                act.activation(hi, land[n % LANDS], ACT.Copy).then_inc(s_split_hi, 1)

            def enter(b):
                yield SLOT["xnt"][0] + 1
                filled["xnt"].wait(act, b)
                filled["tok"].wait_previous(act, b)
                kept_x.wait_previous(act, b)
                act.activation(xh[:, :], bank_of("xnt")[:, :], ACT.Copy).then_inc(xh_ready.sem, 1)
                for j in range(J):
                    yield SLOT["tok"][j] + 1
                    filled["tok"].wait(act, b, j)
                    ps = bank_of("tok", j)
                    yg_ready.wait_previous(act, b, j)
                    act.activation(sz[:, j, :], ps[:, 0:DI], ACT.Silu).then_inc(sz_ready.sem, 1)
                    route_step.wait_previous(act, b)
                    filled["delta"].wait_previous(act, b)
                    act.activation(btd[:, j, :], ps[:, DI:TOK], ACT.Copy).then_inc(btd_ready.sem, 1)
                yield WHEN["dt_exp"][0]
                dt_step.wait(act, b, 1)
                act.activation(dtu[:, :, :], dtv[:, :, :], ACT.Exp).then_inc(dt_exp.sem, 1)
                btd_ready.wait(act, b)
                route_step.wait_previous(act, b)
                act.activation(sig[:, :, :], btd[:, :, N + H:], ACT.Exp, scale=-1.0).then_inc(affexp_ready.sem, 1)
                yield SLOT["cwt"][0] + 1
                filled["cwt"].wait(act, b)
                if not first(b):
                    gate_ready.wait_previous(act, b - 1)
                act.activation(at(CW, b), bank_of("cwt")[:, :], ACT.Copy).then_inc(cw_kept.sem, 1)

            def scan(b):
                for g in range(G):
                    yield SLOT["conv"][g] + 1
                    filled["conv"].wait(act, b, g)
                    tap_done[g].wait_previous(act, b)
                    act.activation(xraw[:, g, K - 1:], bank_of("conv", g)[:, :], ACT.Copy).then_inc(xraw_ready.sem, 1)
                    xraw_ready.wait(act, b, g)
                    filled["xct"].wait_previous(act, b)
                    act.activation(xc[:, g, :], xraw[:, g, 0:T], ACT.Identity, scale=conv_sb[:, g, 0:1])\
                        .then_inc(tap0_done.sem, 1)
                yield SLOT["bc"][0] + 1
                filled["bc"].wait(act, b)
                filled["score"].wait_previous(act, b)
                filled["y"].wait_previous(act, b)
                act.activation(bt[:, :], bank_of("bc")[0:N, :], ACT.Copy).then_inc(bt_ready.sem, 1)
                act.activation(ct[:, :], bank_of("bc")[N:2 * N, :], ACT.Copy, scale=C_SCALE).then_inc(ct_ready.sem, 1)
                def silus():
                    for g in range(G):
                        yield WHEN["xc"][g]
                        tap_done[g].wait(act, b)
                        act.activation(xc[:, g, :], xc[:, g, :], ACT.Silu).then_inc(xc_ready.sem, 1)

                def decays():
                    yield WHEN["decay"][0]
                    filled["cum"].wait(act, b)
                    yint_ready.wait_previous(act, b)
                    stated_ready.wait_previous(act, b)
                    act.activation(grown[:, :, :, :].rearrange("p a j h -> p (a j h)"), bank_of("cum")[:, 0:2 * J * H], ACT.Exp)\
                        .then_inc(grown_ready.sem, 1)
                    mix_ready.wait_previous(act, b)
                    xw_ready.wait_previous(act, b)
                    for j in range(J):
                        filled["between"].wait(act, b, j)
                        act.activation(decay[:, j, :, :].rearrange("p h t -> p (h t)"), bank_of("between", j)[:, :], ACT.Exp)\
                            .then_inc(decay_ready.sem, 1)

                yield from merge(decays(), silus())

                def transposed(j):
                    filled["ygt"].wait(act, b, j)
                    (filled["outp"].wait(act, b, j - 2) if j >= 2 else filled["outp"].wait_previous(act, b, J - 2 + j))
                    act.activation(ygt[:, j % 2, :], bank_of("ygt", j)[:, 0:DI], ACT.Copy).then_inc(ygt_ready.sem, 1)

                for j in range(J):
                    yield SLOT["y"][j] + 2
                    y_ready.wait(act, b, j)
                    if j:
                        ss_ready.wait(act, b, j - 1)
                    rs_ready.wait_previous(act, b)
                    act.activation(yint[:, j % 2, :], y[:, j % 2, :], ACT.Square, accum_out=ss[:, j:j + 1])\
                        .then_inc(ss_ready.sem, 1)
                    if j:
                        yield SLOT["ygt"][j - 1] + 1
                        transposed(j - 1)
                yield SLOT["ygt"][J - 1] + 1
                transposed(J - 1)

            def activate(b, p):
                u_filled.wait(act, b, p)
                if p < NP:
                    after(prod_ready, act, b, p - HIDS)
                    act.activation(hid[:, p % HIDS, :], bank[U_BANK[p % len(U_BANK)]][:, :], ACT.Silu).then_inc(u_read.sem, 1)
                else:
                    after_low(act, b, p)
                    act.activation(prod[0:F, p % DEPTH, :], bank[U_BANK[p % len(U_BANK)]][0:F, :], ACT.Silu).then_inc(u_read.sem, 1)

            def high(b, p):
                n = P if p < NP else F
                (prod_ready if p < NP else u_read).wait(act, b, p)
                after(down_done, act, b, p - DEPTH)
                act.activation(ph[0:n, p % DEPTH, :], prod[0:n, p % DEPTH, :], ACT.Copy).then_inc(high_ready["act"].sem, 1)

            def experts(b, mixer):
                for p in range(NQ):
                    if p:
                        activate(b, p)
                    if p and p - 1 not in DVE_HIGHS:
                        high(b, p - 1)
                    mixer.advance(p)
                if NP not in DVE_HIGHS:
                    high(b, NP)
                mixer.advance(LAST)
                down_done.wait(act, b)
                g_filled.wait_previous(act, b)
                act.activation(gate_t[:, :], bank[Y_BANK][:, :], ACT.Silu).then_inc(gate_ready.sem, 1)

            mixer = Mixer(enter(0))
            mixer.advance(SLOT["xnt"][0] + 1)
            act.wait_ge(ws_up_landed, 16)
            act.activation(up_hi[:, NP, 0:F], land_su, ACT.Copy).then_inc(s_split_hi, 1)
            act.wait_ge(ws_down_landed, 16)
            act.activation(dn_hi[0:F, NP, :], land_sd, ACT.Copy).then_inc(s_split_hi, 1)
            act.wait_ge(s_const, CONSTANTS)
            act.activation(later[:, :], upper[:, :], ACT.Copy, scale=-1.0, bias=1.0).then_inc(s_setup, 1)
            act.wait_ge(rows_landed, 16)
            act.activation(neg_a[:, :], rows_sb[:, E + 4:E + 8], ACT.Exp).then_inc(s_setup, 1)
            act.wait_ge(conv_landed, 16)
            for n, (src, hi, lo) in enumerate(SPLITS):
                split_high(n, src, hi)
                mixer.advance(SPLIT_SLOT[n])
            mixer.advance(LAST)
            wait_up_splits(act)
            activate(0, 0)
            wait_splits(act)
            with act.Fori(0, NB - 1) as b:
                experts(b, Mixer(merge(scan(b), enter(b + 1))))
                activate(b + 1, 0)
            experts(NB - 1, Mixer(scan(NB - 1)))

        @block.vector
        def _(dve):
            for s in (stats_ready, xn_ready, xl_ready, *tap_done, dt_step, biased_ready,
                      top8_ready, replaced_ready, route_step, smask_ready, xdt_ready, yint_ready, y_ready,
                      state_ready, s_kept, da_step, cw_part, prod_ready, low_ready["dve"], high_ready["dve"],
                      fin_step, fin_read):
                s.start(dve)
            def enter(b):
                yield WHEN["stats"][0]
                dve.wait_ge(x_landed, b * 16 + 16)
                rstd_ready.wait_previous(dve, b)
                for j in range(J):
                    dve.bn_stats(stats[:, j, :], x_tok[:, j, :]).then_inc(stats_ready.sem, 1)
                stats_ready.wait(dve, b, J - 1)
                apart(dve)
                for j in range(J):
                    dve.bn_aggr(mv[:, j, :], stats[:, j, :]).then_inc(stats_ready.sem, 1)
                stats_ready.wait(dve, b)
                yield WHEN["xn"][0]
                rstd_ready.wait(dve, b)
                for j in range(J):
                    dve.tensor_scalar(x_tok[:, j, :], x_tok[:, j, :], mv[:, j, 0:1], rstd[:, j:j + 1],
                                      ALU.subtract, ALU.mult).then_inc(xn_ready.sem, 1)
                yield WHEN["xl"][0]
                xh_ready.wait(dve, b)
                filled["tok"].wait_previous(dve, b)
                kept_x.wait_previous(dve, b)
                dve.tensor_tensor(xl[:, :], bank_of("xnt")[:, :], xh[:, :].bitcast(F32), ALU.subtract).then_inc(xl_ready.sem, 1)

                yield WHEN["dt"][0]
                btd_ready.wait(dve, b)
                dt_exp.wait_previous(dve, b)
                dve.tensor_tensor(dtv[:, :, :], btd[:, :, N:N + H],
                                  rows_sb[:, E:E + H].unsqueeze(1).to_broadcast([P, J, H]), ALU.add).then_inc(dt_step.sem, 1)
                dt_step.wait(dve, b, 0)
                dve.tensor_scalar(dtv[:, :, :], dtv[:, :, :], DT_CAP, None, ALU.min).then_inc(dt_step.sem, 1)

                def time_steps():
                    yield WHEN["dt_rest"][0]
                    dt_exp.wait(dve, b)
                    dve.tensor_scalar(dtr[:, :, :], dtu[:, :, :], 2.0, 0.5, ALU.add, ALU.mult).then_inc(dt_step.sem, 1)
                    dt_step.wait(dve, b, 2)
                    dve.reciprocal(dtr[:, :, :], dtr[:, :, :]).then_inc(dt_step.sem, 1)
                    dt_step.wait(dve, b, 3)
                    dve.tensor_tensor(dts[:, :, :], dtr[:, :, :], dtu[:, :, :], ALU.mult).then_inc(dt_step.sem, 1)
                    dt_step.wait(dve, b, 4)
                    dve.scalar_tensor_tensor(dtq[:, :, :], dts[:, :, :], 0.25, dts[:, :, :], ALU.mult, ALU.mult)\
                        .then_inc(dt_step.sem, 1)
                    dt_step.wait(dve, b, 5)
                    dve.tensor_scalar(dtl[:, :, :], dtq[:, :, :], 1.0 / LN_ODD[0], None, ALU.mult).then_inc(dt_step.sem, 1)
                    for n, odd in enumerate(LN_ODD[1:]):
                        dt_step.wait(dve, b, 6 + n)
                        dve.scalar_tensor_tensor(dtl[:, :, :], dtl[:, :, :], 1.0 / odd, (dtq if odd > 1 else dts)[:, :, :],
                                                 ALU.add, ALU.mult).then_inc(dt_step.sem, 1)
                    dt_step.wait(dve, b, 6 + len(LN_ODD) - 1)
                    xdt_ready.wait_previous(dve, b)
                    dve.tensor_scalar(dt_[:, :, :], dtl[:, :, :], DT_MIN, DT_MAX, ALU.max, ALU.min).then_inc(dt_step.sem, 1)
                    dt_step.wait(dve, b, 6 + len(LN_ODD))
                    filled["cum"].wait_previous(dve, b)
                    spread_ready.wait_previous(dve, b)
                    dve.tensor_tensor(da[:, :, :], dt_[:, :, :], neg_a[:, :].unsqueeze(1).to_broadcast([P, J, H]), ALU.mult)\
                        .then_inc(da_step.sem, 1)
                    da_step.wait(dve, b, 0)
                    dve.tensor_copy(da_hi[:, :, :], da[:, :, :]).then_inc(da_step.sem, 1)
                    da_step.wait(dve, b, 1)
                    dve.tensor_tensor(da_lo[:, :, :], da[:, :, :], da_hi[:, :, :].bitcast(F32), ALU.subtract).then_inc(da_step.sem, 1)
                    dve.sem_inc(dt_step.sem, 1)

                def route():
                    yield WHEN["route"][0]
                    btd_ready.wait(dve, b)
                    replaced_ready.wait_previous(dve, b)
                    dve.tensor_tensor(biased[:, :, :], btd[:, :, N + H:],
                                      rows_sb[:, 0:E].unsqueeze(1).to_broadcast([P, J, E]), ALU.add).then_inc(biased_ready.sem, 1)
                    biased_ready.wait(dve, b)
                    apart(dve)
                    for j in range(J):
                        dve.max(top8[:, j, :], biased[:, j, :]).then_inc(top8_ready.sem, 1)
                    yield WHEN["route"][1]
                    for j in range(J):
                        top8_ready.wait(dve, b, j)
                        apart(dve)
                        dve.match_replace(replaced[:, j, :], top8[:, j, :], biased[:, j, :], LOWEST).then_inc(replaced_ready.sem, 1)

                def sigmoid():
                    yield WHEN["sigmoid"][0]
                    affexp_ready.wait(dve, b)
                    dve.tensor_scalar(sig[:, :, :], sig[:, :, :], 1.0, None, ALU.add).then_inc(route_step.sem, 1)
                    replaced_ready.wait(dve, b)
                    dve.tensor_tensor(replaced[:, :, :], replaced[:, :, :], biased[:, :, :], ALU.not_equal)\
                        .then_inc(route_step.sem, 1)
                    for j in range(J):
                        yield WHEN["sigmoid"][1 + j]
                        route_step.wait(dve, b, 0)
                        dve.reciprocal(sig[:, j, :], sig[:, j, :]).then_inc(route_step.sem, 1)
                    yield WHEN["sigmoid"][1 + J]
                    route_step.wait(dve, b, J + 1)
                    dve.tensor_tensor(sig[:, :, :], sig[:, :, :], replaced[:, :, :], ALU.mult).then_inc(route_step.sem, 1)
                    route_step.wait(dve, b, J + 2)
                    dve.tensor_reduce(wsum[:, :], sig[:, :, :], AX_X, ALU.add).then_inc(route_step.sem, 1)
                    yield WHEN["sigmoid"][2 + J]
                    route_step.wait(dve, b, J + 3)
                    dve.tensor_scalar(wsum[:, :], wsum[:, :], 1e-8, None, ALU.add).then_inc(route_step.sem, 1)
                    route_step.wait(dve, b, J + 4)
                    dve.reciprocal(wrec[:, :], wsum[:, :]).then_inc(route_step.sem, 1)
                    route_step.wait(dve, b, J + 5)
                    dve.tensor_tensor(sig[:, :, :], sig[:, :, :], wrec[:, :].unsqueeze(2).to_broadcast([P, J, E]), ALU.mult)\
                        .then_inc(route_step.sem, 1)
                    yield WHEN["sigmoid"][3 + J]
                    route_step.wait(dve, b, J + 6)
                    filled["cwt"].wait_previous(dve, b)
                    dve.tensor_copy(cw_cat[:, :, 0, :].bitcast(F32R), sig[:, :, :]).then_inc(cw_part.sem, 1)
                    cw_part.wait(dve, b, 0)
                    dve.tensor_tensor(cw_cat[:, :, 1, :], sig[:, :, :], cw_cat[:, :, 0, :], ALU.subtract).then_inc(cw_part.sem, 1)
                    cw_part.wait(dve, b, 1)
                    dve.sem_inc(route_step.sem, 1)

                def choose():
                    yield from route()
                    yield from sigmoid()

                yield from merge(choose(), time_steps())

            def scan(b):
                def convolve(g):
                    for k in range(1, K):
                        yield WHEN["taps"][(K - 1) * g + k - 1]
                        tap_done[g].wait(dve, b, k - 2) if k > 1 else tap0_done.wait(dve, b, g)
                        dve.scalar_tensor_tensor(xc[:, g, :], xraw[:, g, k:k + T], conv_sb[:, g, k:k + 1], xc[:, g, :],
                                                 ALU.mult, ALU.add).then_inc(tap_done[g].sem, 1)

                yield from merge(convolve(0), convolve(1))

                def chunk_inputs(j):
                    q = j % 2
                    filled["xct"].wait(dve, b, j)
                    (filled["y"].wait(dve, b, j - 2) if j >= 2 else filled["y"].wait_previous(dve, b, J - 2 + j))
                    (xw_ready.wait(dve, b, j - 2) if j >= 2 else xw_ready.wait_previous(dve, b, J - 2 + j))
                    dve.tensor_tensor(xdt[:, q, :].rearrange("p (h n) -> p h n", h=H),
                                      bank_of("xct", j)[:, 0:DI].rearrange("p (h n) -> p h n", h=H),
                                      dt_[:, j, :].unsqueeze(2).to_broadcast([P, H, HP]), ALU.mult).then_inc(xdt_ready.sem, 1)
                    filled["score"].wait(dve, b, j)
                    (mix_ready.wait(dve, b, j - 2) if j >= 2 else mix_ready.wait_previous(dve, b, J - 2 + j))
                    dve.tensor_tensor(smask[:, q, :], bank_of("score", j)[:, 0:P], upper[:, :], ALU.mult).then_inc(smask_ready.sem, 1)

                def output(j):
                    filled["outp"].wait(dve, b, j)
                    rs_ready.wait(dve, b, 2 * j + 1)
                    fin_read.wait_previous(dve, b)
                    dve.tensor_scalar(S[:, j * D:(j + 1) * D], bank_of("outp", j)[:, 0:D], rs[:, j:j + 1], None, ALU.mult)\
                        .then_inc(s_kept.sem, 1)

                for j in range(2):
                    yield SLOT["xct"][j] + 1
                    chunk_inputs(j)
                for j in range(J):
                    q = j % 2
                    yield SLOT["y"][j] + 1
                    filled["y"].wait(dve, b, j)
                    ps = bank_of("y", j)
                    if j >= 2:
                        yg_ready.wait(dve, b, j - 2)
                        ss_ready.wait(dve, b, j - 2)
                    else:
                        yg_ready.wait_previous(dve, b, J - 2 + j)
                        ss_ready.wait_previous(dve, b, J - 2 + j)
                    if j:
                        grown_ready.wait(dve, b)
                        dve.tensor_tensor(yint[:, q, :].rearrange("p (h n) -> p h n", h=H),
                                          ps[:, DI:2 * DI].rearrange("p (h n) -> p h n", h=H),
                                          grown[:, 0, j, :].unsqueeze(2).to_broadcast([P, H, HP]), ALU.mult).then_inc(yint_ready.sem, 1)
                        yint_ready.wait(dve, b, j)
                        dve.tensor_tensor(y[:, q, :], ps[:, 0:DI], yint[:, q, :], ALU.add).then_inc(y_ready.sem, 1)
                    else:
                        dve.sem_inc(yint_ready.sem, 1)
                        dve.tensor_copy(y[:, q, :], ps[:, 0:DI]).then_inc(y_ready.sem, 1)
                    if j + 1 < J:
                        filled["delta"].wait(dve, b, j)
                        if j == 0:
                            filled["y"].wait_previous(dve, b)
                            stated_ready.wait_previous(dve, b)
                            dve.tensor_copy(state[:, 0, :], bank_of("delta", j)[0:N, 0:DI]).then_inc(state_ready.sem, 1)
                        else:
                            stated_ready.wait(dve, b, j - 1)
                            dve.tensor_tensor(state[:, j, :], bank_of("delta", j)[0:N, 0:DI], state_d[:, j - 1, :], ALU.add)\
                                .then_inc(state_ready.sem, 1)
                    if j:
                        yield SLOT["outp"][j - 1] + 1
                        output(j - 1)
                    if j + 2 < J:
                        yield SLOT["xct"][j + 2] + 1
                        chunk_inputs(j + 2)
                yield SLOT["outp"][J - 1] + 1
                output(J - 1)
                dve.sem_inc(state_ready.sem, 1)

            def weigh(b, p):
                u_read.wait(dve, b, p)
                c_filled.wait(dve, b, p)
                after_low(dve, b, p)
                dve.tensor_tensor(prod[:, p % DEPTH, :], hid[:, p % HIDS, :], bank[C_BANK[p % len(C_BANK)]][:, :], ALU.mult)\
                    .then_inc(prod_ready.sem, 1)

            def parts(b, p):
                if p in DVE_HIGHS:
                    n = P if p < NP else F
                    (prod_ready if p < NP else u_read).wait(dve, b, p)
                    after(down_done, dve, b, p - DEPTH)
                    dve.tensor_copy(ph[0:n, p % DEPTH, :], prod[0:n, p % DEPTH, :]).then_inc(high_ready["dve"].sem, 1)
                if p not in POOL_LOWS:
                    take_low(dve, b, p)

            def experts(b, mixer):
                for p in range(NP):
                    if p:
                        weigh(b, p)
                        parts(b, p - 1)
                    mixer.advance(p)
                parts(b, NP - 1)
                parts(b, NP)
                mixer.advance(LAST)

            def finish(b):
                s_kept.wait(dve, b)
                g_filled.wait(dve, b)
                dve.tensor_tensor(S[:, :], S[:, :], bank[Y_BANK][:, :], ALU.mult)\
                    .then_inc(fin_step.sem, 1)

            mixer = Mixer(enter(0))
            mixer.advance(max(WHEN["stats"][0], WHEN["xn"][0]))
            for n, (whole, hi, lo) in enumerate(((land_proj, wp_hi[:, :], wp_lo[:, :]),
                                                 (land_su, up_hi[:, NP, 0:F], up_lo[:, NP, 0:F]),
                                                 (land_sd, dn_hi[0:F, NP, :], dn_lo[0:F, NP, :]))):
                dve.wait_ge(s_split_hi, n + 1)
                dve.tensor_tensor(lo, whole, hi.bitcast(F32), ALU.subtract).then_inc(s_split_lo, 1)
                mixer.advance(WHEN["xl"][0])
            dve.wait_ge(s_setup, 2)
            dve.tensor_scalar(neg_a[:, :], neg_a[:, :], -1.0, None, ALU.mult).then_inc(s_setup, 1)
            dve.wait_ge(s_setup, 3)
            dve.wait_ge(conv_landed, 16)
            for n, (src, hi, lo) in enumerate(SPLITS):
                if n not in POOL_SPLITS:
                    split_low(dve, n)
                mixer.advance(SPLIT_SLOT[n])
            mixer.advance(LAST)
            wait_up_splits(dve)
            weigh(0, 0)
            with dve.Fori(0, NB - 1) as b:
                experts(b, Mixer(merge(scan(b), enter(b + 1))))
                weigh(b + 1, 0)
                finish(b)
            experts(NB - 1, Mixer(scan(NB - 1)))
            finish(NB - 1)

        @block.tensor
        def _(pe):
            for s in (*filled.values(), u_filled, c_filled, down_done, g_filled):
                s.start(pe)

            def mm3(out_, lhs_hi, lhs_lo, rhs_hi, rhs_lo, start=True, stop=True):
                pe.matmul(out_, lhs_hi, rhs_lo, start=start, stop=False)
                pe.matmul(out_, lhs_lo, rhs_hi, start=False, stop=False)
                return pe.matmul(out_, lhs_hi, rhs_hi, start=False, stop=stop)

            pe.wait_ge(s_const, CONSTANTS)

            def enter(b, alone=False):
                yield SLOT["xnt"][0]
                wait_bank(pe, b, "xnt", 0, alone)
                for j in range(J):
                    xn_ready.wait(pe, b, j)
                    last = pe.transpose(bank_of("xnt")[:, j * P:(j + 1) * P], x_tok[:, j, :], ident[:, :])
                last.then_inc(filled["xnt"].sem, 1)
                if alone:
                    pe.wait_ge(s_split_lo, 1)
                for j in range(J):
                    yield SLOT["tok"][j]
                    xh_ready.wait(pe, b)
                    xl_ready.wait(pe, b)
                    wait_bank(pe, b, "tok", j, alone)
                    t = slice(j * P, (j + 1) * P)
                    mm3(bank_of("tok", j)[:, 0:TOK], xh[:, t], xl[:, t], wp_hi[:, 0:TOK], wp_lo[:, 0:TOK])\
                        .then_inc(filled["tok"].sem, 1)
                yield SLOT["cwt"][0]
                wait_bank(pe, b, "cwt", 0, alone)
                cw_part.wait(pe, b)
                for j in range(J):
                    last = pe.transpose(bank_of("cwt")[:, j * P:(j + 1) * P],
                                        cw_cat[:, j, :, :].rearrange("p a e -> p (a e)"), ident[:, :])
                last.then_inc(filled["cwt"].sem, 1)

            def scan(b, alone=False):
                for g in range(G):
                    yield SLOT["conv"][g]
                    wait_bank(pe, b, "conv", g, alone)
                    c = slice(C_CONV + g * P, C_CONV + (g + 1) * P)
                    mm3(bank_of("conv", g)[:, :], wp_hi[:, c], wp_lo[:, c], at(XH, b), at(XL, b)).then_inc(filled["conv"].sem, 1)
                yield SLOT["bc"][0]
                wait_bank(pe, b, "bc", 0, alone)
                c = slice(C_BC, C_BC + 2 * N)
                mm3(bank_of("bc")[:, :], wp_hi[:, c], wp_lo[:, c], at(XH, b), at(XL, b)).then_inc(filled["bc"].sem, 1)

                yield SLOT["cum"][0]
                wait_bank(pe, b, "cum", 0, alone)
                da_step.wait(pe, b)
                da_flat = da[:, :, :].rearrange("p j h -> p (j h)")
                pe.matmul(bank_of("cum")[:, 0:J * H], upper[:, :], da_flat, start=True, stop=True)
                pe.matmul(bank_of("cum")[:, J * H:2 * J * H], ones[:, :], da_flat, start=True, stop=True)\
                    .then_inc(filled["cum"].sem, 1)
                for j in range(J):
                    yield SLOT["between"][j]
                    wait_bank(pe, b, "between", j, alone)
                    spread_ready.wait(pe, b, 2 * j + 1)
                    o = bank_of("between", j)[:, :]
                    pe.matmul(o, later[:, :], spread_lo[:, j % 2, :, :].rearrange("p h t -> p (h t)"), start=True, stop=False)
                    pe.matmul(o, later[:, :], spread_hi[:, j % 2, :, :].rearrange("p h t -> p (h t)"), start=False, stop=True)\
                        .then_inc(filled["between"].sem, 1)

                def chunk_inputs(j):
                    t = slice(j * P, (j + 1) * P)
                    wait_bank(pe, b, "xct", j, alone)
                    for g in range(G):
                        xc_ready.wait(pe, b, g)
                        last = pe.transpose(bank_of("xct", j)[:, g * P:(g + 1) * P], xc[:, g, t], ident[:, :])
                    last.then_inc(filled["xct"].sem, 1)
                    wait_bank(pe, b, "score", j, alone)
                    bt_ready.wait(pe, b)
                    ct_ready.wait(pe, b)
                    pe.matmul(bank_of("score", j)[:, 0:P], bt[:, t], ct[:, t], start=True, stop=True)\
                        .then_inc(filled["score"].sem, 1)

                def gated_transpose(j):
                    q = j % 2
                    wait_bank(pe, b, "ygt", j, alone)
                    yg_ready.wait(pe, b, j)
                    for g in range(G):
                        last = pe.transpose(bank_of("ygt", j)[:, g * P:(g + 1) * P], yg[:, q, g * P:(g + 1) * P], ident[:, :])
                    last.then_inc(filled["ygt"].sem, 1)

                def project(j):
                    q = j % 2
                    wait_bank(pe, b, "outp", j, alone)
                    ygt_ready.wait(pe, b, j)
                    for g in range(G):
                        last = pe.matmul(bank_of("outp", j)[:, 0:D], ygt[:, q, g * P:(g + 1) * P], w_out_sb[:, g, :],
                                         start=(g == 0), stop=(g == G - 1))
                    last.then_inc(filled["outp"].sem, 1)

                for j in range(2):
                    yield SLOT["xct"][j]
                    chunk_inputs(j)
                for j in range(J):
                    q = j % 2
                    t = slice(j * P, (j + 1) * P)
                    yield SLOT["y"][j]
                    wait_bank(pe, b, "y", j, alone)
                    xdt_ready.wait(pe, b, j)
                    mix_ready.wait(pe, b, j)
                    ps = bank_of("y", j)
                    for h in range(H):
                        last = pe.matmul(ps[:, h * HP:(h + 1) * HP], mix[:, q, h, :], xdt[:, q, h * HP:(h + 1) * HP],
                                         start=True, stop=True)
                    if j:
                        state_ready.wait(pe, b, j - 1)
                        last = pe.matmul(ps[:, DI:2 * DI], ct[:, t], state[:, j - 1, :], start=True, stop=True)
                    last.then_inc(filled["y"].sem, 1)
                    if j + 1 < J:
                        wait_bank(pe, b, "delta", j, alone)
                        xw_ready.wait(pe, b, j)
                        pe.matmul(bank_of("delta", j)[0:N, 0:DI], btd[:, j, 0:N], xw[:, q, :], start=True, stop=True)\
                            .then_inc(filled["delta"].sem, 1)
                    if j:
                        yield SLOT["ygt"][j - 1]
                        gated_transpose(j - 1)
                        yield SLOT["outp"][j - 1]
                        project(j - 1)
                    if j + 2 < J:
                        yield SLOT["xct"][j + 2]
                        chunk_inputs(j + 2)
                yield SLOT["ygt"][J - 1]
                gated_transpose(J - 1)
                yield SLOT["outp"][J - 1]
                project(J - 1)

            def up(b, p):
                after(u_read, pe, b, p - len(U_BANK))
                n = P if p < NP else F
                if p == NP:
                    apart(pe)
                mm3(bank[U_BANK[p % len(U_BANK)]][0:n, :], up_hi[:, p, 0:n], up_lo[:, p, 0:n], at(XH, b), at(XL, b))\
                    .then_inc(u_filled.sem, 1)

            def weights(b, p):
                after(prod_ready, pe, b, p - len(C_BANK))
                pe.matmul(bank[C_BANK[p % len(C_BANK)]][:, :], stair[:, 2 * p:2 * p + 2, :].rearrange("p e f -> p (e f)"),
                          at(CW, b), start=True, stop=True).then_inc(c_filled.sem, 1)

            def down(b, p):
                wait_high(pe, b, p)
                wait_low(pe, b, p)
                if p == 0:
                    fin_step.wait_previous(pe, b, 0)
                n = P if p < NP else F
                mm3(bank[Y_BANK][:, :], dn_hi[0:n, p, :], dn_lo[0:n, p, :], ph[0:n, p % DEPTH, :], pl[0:n, p % DEPTH, :],
                    start=(p == 0), stop=(p == NP)).then_inc(down_done.sem, 1)

            def experts(b, mixer):
                for p in range(max(DOWN_SLOT) + 1):
                    if p + len(U_BANK) < NQ:
                        up(b, p + len(U_BANK))
                    if p + C_LEAD < NP:
                        weights(b, p + C_LEAD)
                    for q in range(NQ):
                        if DOWN_SLOT[q] == p:
                            down(b, q)
                    mixer.advance(p)
                mixer.advance(LAST)

            def begin(b):
                kept_x.wait(pe, b)
                for p in range(len(U_BANK)):
                    up(b, p)
                cw_kept.wait(pe, b)
                for p in range(C_LEAD):
                    weights(b, p)

            def gate(b):
                gate_ready.wait(pe, b)
                for j in range(J):
                    last = pe.transpose(bank[Y_BANK][:, j * P:(j + 1) * P], gate_t[:, j * P:(j + 1) * P], ident[:, :])
                last.then_inc(g_filled.sem, 1)

            run(enter(0, alone=True))
            wait_up_splits(pe)
            pe.wait_ge(s_stair, 3)
            begin(0)
            wait_splits(pe)
            pe.wait_ge(s_setup, 3)
            pe.wait_ge(w_out_landed, 16)
            with pe.Fori(0, NB - 1) as b:
                experts(b, Mixer(merge(scan(b), enter(b + 1))))
                begin(b + 1)
                gate(b)
            experts(NB - 1, Mixer(scan(NB - 1, alone=True)))
            gate(NB - 1)


def kernel(**inputs):
    import numpy as np
    import concourse.bacc as bacc
    from concourse.bass_utils import run_bass_kernel_spmd

    a = {k: np.asarray(v) for k, v in inputs.items()}
    w_in = a["L0_attn_W_in"].T
    w_out = a["L0_attn_W_out"].T
    cent = a["L0_ffn_centroids"].T
    D, DI = w_in.shape[0], w_out.shape[0]
    E, _, F = a["L0_ffn_W_up"].shape
    H = a["L0_attn_A_log"].shape[0]
    N = (w_in.shape[1] - 2 * DI - H) // 2
    z, xc, B, C, dt = np.split(w_in, [DI, 2 * DI, 2 * DI + N, 2 * DI + 2 * N], axis=1)
    row = np.concatenate([a["L0_ffn_expert_biases"], a["L0_attn_dt_bias"], a["L0_attn_A_log"]])
    arrays = {
        "x": a["L0_attn_x"],
        "w_proj": np.concatenate([z, B, dt, cent, xc, B, C], axis=1),
        "w_out_t": w_out.reshape(DI // 128, 128, D).transpose(1, 0, 2),
        "conv_w": a["L0_attn_conv_w"].reshape(DI // 128, 128, -1).transpose(1, 0, 2),
        "rows": np.broadcast_to(row, (128, row.size)),
        "w_up": a["L0_ffn_W_up"].transpose(1, 0, 2).reshape(D, E * F),
        "w_down": a["L0_ffn_W_down"].reshape(E // 2, 2 * F, D).transpose(1, 0, 2).reshape(2 * F, (E // 2) * D),
        "ws_up": a["L0_ffn_Ws_up"],
        "ws_down": a["L0_ffn_Ws_down"],
    }
    arrays = {k: np.ascontiguousarray(v) for k, v in arrays.items()}
    nc = bacc.Bacc("TRN2", target_bir_lowering=False, num_devices=1)
    args = [nc.dram_tensor(k, v.shape, F32, kind="ExternalInput").ap() for k, v in arrays.items()]
    out = nc.dram_tensor("out", a["L0_attn_x"].shape, F32, kind="ExternalOutput").ap()
    build(nc, *args, out)
    r = run_bass_kernel_spmd(nc, [arrays], core_ids=[0])
    return r.results[0]["out"]
```
